# Optimizing a Trainium2 kernel written in Bass

```python
import numpy as np
import jax
import jax.numpy as jnp

def _softmax(x, axis=-1):
    return jax.nn.softmax(x, axis=axis)

def _gelu(x):
    return jax.nn.gelu(x, approximate=True)

def _silu(x):
    return jax.nn.silu(x)

def _sigmoid(x):
    return jax.nn.sigmoid(x)

def _layernorm(x, axis=-1, eps=1e-05):
    m = jnp.mean(x, axis=axis, keepdims=True)
    v = jnp.var(x, axis=axis, keepdims=True)
    return (x - m) / jnp.sqrt(v + eps)

def _scatter_add(tgt, idx, src, axis=0):
    return tgt.at[idx].add(src)

def _segment_sum(src, seg, n):
    return jax.ops.segment_sum(src, seg, n)
kernel_name = 'mk_conv_attn_hybrid_d2_conv_nchw128_r4_58730a'

def setup_inputs(seed: int=0):
    np.random.seed(seed)
    _w = jnp.asarray

    def _rec_inputs():
        import jax
        import jax.numpy as jnp
        _gk = jax.random.key(seed)
        x = -0.0002928 + 1 * jax.random.normal(jax.random.fold_in(_gk, 1), (8, 32, 16, 16), jnp.float32)
        return x
    x = _rec_inputs()

    def _L0_conv_setup():
        import jax, jax.numpy as jnp
        from jax import lax
        import numpy as np
        EPS = 1e-05

        def ref_points(Hk, Wk):
            ys = jnp.linspace(0.5, Hk - 0.5, Hk) / Hk * 2.0 - 1.0
            xs = jnp.linspace(0.5, Wk - 0.5, Wk) / Wk * 2.0 - 1.0
            yy, xx = jnp.meshgrid(ys, xs, indexing='ij')
            return jnp.stack([yy, xx], axis=-1)

        def grid_sample(img, grid):
            N, C, Hi, Wi = img.shape
            Hg, Wg = (grid.shape[1], grid.shape[2])
            gx = (grid[..., 0] + 1.0) * 0.5 * (Wi - 1)
            gy = (grid[..., 1] + 1.0) * 0.5 * (Hi - 1)
            x0 = jnp.floor(gx)
            y0 = jnp.floor(gy)
            wx1 = gx - x0
            wy1 = gy - y0
            imgf = img.reshape(N, C, Hi * Wi)

            def corner(ix, iy, w):
                valid = (ix >= 0) & (ix < Wi) & (iy >= 0) & (iy < Hi)
                idx = (jnp.clip(iy, 0, Hi - 1).astype(jnp.int32) * Wi + jnp.clip(ix, 0, Wi - 1).astype(jnp.int32)).reshape(N, -1)
                vals = jax.vmap(lambda im, f: im[:, f])(imgf, idx)
                return vals * (w * valid).reshape(N, 1, -1)
            out = corner(x0, y0, (1 - wx1) * (1 - wy1)) + corner(x0 + 1, y0, wx1 * (1 - wy1)) + corner(x0, y0 + 1, (1 - wx1) * wy1) + corner(x0 + 1, y0 + 1, wx1 * wy1)
            return out.reshape(N, C, Hg, Wg)
        key = jax.random.key(seed)
        ks = jax.random.split(key, 8)
        B, C, H, W = (8, 32, 16, 16)
        gc, nH = (16, 4)
        return {'x': jax.random.normal(ks[0], (B, C, H, W), jnp.float32), 'w_dw': jax.random.normal(ks[1], (gc, 1, 5, 5), jnp.float32) * 0.1, 'ln_w': jnp.ones((gc,), jnp.float32), 'w_off': jax.random.normal(ks[2], (3, gc), jnp.float32) * 0.1, 'wq': jax.random.normal(ks[3], (C, C), jnp.float32) * 0.05, 'wk': jax.random.normal(ks[4], (C, C), jnp.float32) * 0.05, 'wv': jax.random.normal(ks[5], (C, C), jnp.float32) * 0.05, 'wo': jax.random.normal(ks[6], (C, C), jnp.float32) * 0.05, 'rpe': jax.random.normal(ks[7], (nH, 2 * H - 1, 2 * W - 1), jnp.float32) * 0.01}
    _L0_conv_all = _L0_conv_setup()
    _L0_conv_in = {k: v for k, v in _L0_conv_all.items() if k in ('w_dw', 'ln_w', 'w_off', 'wq', 'wk', 'wv', 'wo', 'rpe')}
    del _L0_conv_all

    def _L1_attn_setup():
        import jax, jax.numpy as jnp
        import numpy as np
        key = jax.random.key(seed)
        inputs = jax.random.normal(key, (4, 1024, 32), dtype=jnp.float32)
        return {'inputs': inputs}
    _L1_attn_all = _L1_attn_setup()
    _L1_attn_in = {k: v for k, v in _L1_attn_all.items() if k in ()}
    del _L1_attn_all

    def _L1_ffn_setup():
        import jax, jax.numpy as jnp
        import numpy as np
        B, S, D, E, H, O, K = (128, 512, 32, 16, 128, 32, 8)
        key = jax.random.key(seed)
        k0, k1, k2, k3 = jax.random.split(key, 4)
        x = jax.random.normal(k0, (B, S, D), dtype=jnp.float32)
        gate_w = jax.random.normal(k1, (E, D), dtype=jnp.float32) * (1.0 / np.sqrt(D))
        gate_b = jnp.zeros((E,), dtype=jnp.float32)
        weight1 = jax.random.uniform(k2, (E, D + 1, H), dtype=jnp.float32, minval=-1.0, maxval=1.0) * (1.0 / np.sqrt(D + 1))
        weight2 = jax.random.uniform(k3, (E, H + 1, O), dtype=jnp.float32, minval=-1.0, maxval=1.0) * (1.0 / np.sqrt(H + 1))
        return {'x': x, 'gate_w': gate_w, 'gate_b': gate_b, 'weight1': weight1, 'weight2': weight2}
    _L1_ffn_all = _L1_ffn_setup()
    _L1_ffn_in = {k: v for k, v in _L1_ffn_all.items() if k in ('gate_w', 'gate_b', 'weight1', 'weight2')}
    del _L1_ffn_all
    return {'x': x, 'L0_conv_w_dw': _L0_conv_in['w_dw'], 'L0_conv_ln_w': _L0_conv_in['ln_w'], 'L0_conv_w_off': _L0_conv_in['w_off'], 'L0_conv_wq': _L0_conv_in['wq'], 'L0_conv_wk': _L0_conv_in['wk'], 'L0_conv_wv': _L0_conv_in['wv'], 'L0_conv_wo': _L0_conv_in['wo'], 'L0_conv_rpe': _L0_conv_in['rpe'], 'L1_ffn_gate_w': _L1_ffn_in['gate_w'], 'L1_ffn_gate_b': _L1_ffn_in['gate_b'], 'L1_ffn_weight1': _L1_ffn_in['weight1'], 'L1_ffn_weight2': _L1_ffn_in['weight2']}

def reference(x, L0_conv_w_dw, L0_conv_ln_w, L0_conv_w_off, L0_conv_wq, L0_conv_wk, L0_conv_wv, L0_conv_wo, L0_conv_rpe, L1_ffn_gate_w, L1_ffn_gate_b, L1_ffn_weight1, L1_ffn_weight2):
    import jax
    import jax.numpy as jnp

    def _L0_conv_ref(x, w_dw, ln_w, w_off, wq, wk, wv, wo, rpe):
        import jax, jax.numpy as jnp
        from jax import lax
        import numpy as np
        EPS = 1e-05

        def ref_points(Hk, Wk):
            ys = jnp.linspace(0.5, Hk - 0.5, Hk) / Hk * 2.0 - 1.0
            xs = jnp.linspace(0.5, Wk - 0.5, Wk) / Wk * 2.0 - 1.0
            yy, xx = jnp.meshgrid(ys, xs, indexing='ij')
            return jnp.stack([yy, xx], axis=-1)

        def grid_sample(img, grid):
            N, C, Hi, Wi = img.shape
            Hg, Wg = (grid.shape[1], grid.shape[2])
            gx = (grid[..., 0] + 1.0) * 0.5 * (Wi - 1)
            gy = (grid[..., 1] + 1.0) * 0.5 * (Hi - 1)
            x0 = jnp.floor(gx)
            y0 = jnp.floor(gy)
            wx1 = gx - x0
            wy1 = gy - y0
            imgf = img.reshape(N, C, Hi * Wi)

            def corner(ix, iy, w):
                valid = (ix >= 0) & (ix < Wi) & (iy >= 0) & (iy < Hi)
                idx = (jnp.clip(iy, 0, Hi - 1).astype(jnp.int32) * Wi + jnp.clip(ix, 0, Wi - 1).astype(jnp.int32)).reshape(N, -1)
                vals = jax.vmap(lambda im, f: im[:, f])(imgf, idx)
                return vals * (w * valid).reshape(N, 1, -1)
            out = corner(x0, y0, (1 - wx1) * (1 - wy1)) + corner(x0 + 1, y0, wx1 * (1 - wy1)) + corner(x0, y0 + 1, (1 - wx1) * wy1) + corner(x0 + 1, y0 + 1, wx1 * wy1)
            return out.reshape(N, C, Hg, Wg)
        B, C, H, W = x.shape
        G, nH = (2, 4)
        gc = C // G
        dh = C // nH
        gh = nH // G
        scale = dh ** (-0.5)
        orf = 1.0
        conv1x1 = lambda t, w: jnp.einsum('oi,bihw->bohw', w, t)
        q = conv1x1(x, wq)
        q_off = q.reshape(B * G, gc, H, W)
        off = lax.conv_general_dilated(q_off, w_dw, (4, 4), ((2, 2), (2, 2)), dimension_numbers=('NCHW', 'OIHW', 'NCHW'), feature_group_count=gc)
        var = jnp.var(off, axis=1, keepdims=True)
        off = off / jnp.sqrt(var + EPS) * ln_w.reshape(1, -1, 1, 1)
        off = jax.nn.gelu(off, approximate=False)
        off = jnp.einsum('oi,bihw->bohw', w_off, off)
        Hk, Wk = (off.shape[2], off.shape[3])
        n = Hk * Wk
        offset = jnp.stack([jnp.tanh(off[:, 0]) * (orf / Hk), jnp.tanh(off[:, 1]) * (orf / Wk)], axis=-1)
        dm = jax.nn.sigmoid(off[:, 2])[:, None]
        pos = offset + ref_points(Hk, Wk)[None]
        xs = grid_sample(x.reshape(B * G, gc, H, W), pos[..., ::-1])
        xs = (xs * dm).reshape(B, C, 1, n)
        k = conv1x1(xs, wk).reshape(B * nH, dh, n)
        v = conv1x1(xs, wv).reshape(B * nH, dh, n)
        qf = q.reshape(B * nH, dh, H * W)
        attn = jnp.einsum('bcm,bcn->bmn', qf, k) * scale
        rpe_b = jnp.broadcast_to(rpe[None], (B, nH, 2 * H - 1, 2 * W - 1)).reshape(B * G, gh, 2 * H - 1, 2 * W - 1)
        qg = ref_points(H, W).reshape(H * W, 2)
        disp = (qg[None, :, None, :] - pos.reshape(B * G, 1, n, 2)) * 0.5
        bias = grid_sample(rpe_b, disp[..., ::-1]).reshape(B * nH, H * W, n)
        attn = jax.nn.softmax(attn + bias, axis=2)
        out = jnp.einsum('bmn,bcn->bcm', attn, v).reshape(B, C, H, W)
        return conv1x1(out, wo)

    def _L1_attn_ref(inputs):
        import jax, jax.numpy as jnp
        import numpy as np
        scores = jnp.einsum('bqd,bkd->bqk', inputs, inputs)
        weights = jax.nn.softmax(scores, axis=-1)
        out = jnp.einsum('bqk,bkd->bqd', weights, inputs)
        return out

    def _L1_ffn_ref(x, gate_w, gate_b, weight1, weight2):
        import jax, jax.numpy as jnp
        import numpy as np
        B, S, D, E, H, O, K = (128, 512, 32, 16, 128, 32, 8)
        Bn, Sn, Dn = x.shape
        logits = jnp.einsum('bsd,ed->bse', x, gate_w) + gate_b
        probs = jax.nn.softmax(logits, axis=1)
        vals, idx = jax.lax.top_k(probs.transpose(0, 2, 1), K)
        topv = vals.transpose(0, 2, 1)
        topi = idx.transpose(0, 2, 1)
        flat_idx = topi.reshape(Bn, K * E)
        gathered = jnp.take_along_axis(x, flat_idx[:, :, None], axis=1)
        gathered = gathered.reshape(Bn, K, E, Dn)
        pooled = jnp.einsum('bked,bke->bed', gathered, topv)
        ones = jnp.ones((E, Bn, 1), dtype=x.dtype)
        h = jnp.concatenate([pooled.transpose(1, 0, 2), ones], axis=-1)
        h = jax.nn.gelu(jnp.einsum('ebd,edh->ebh', h, weight1), approximate=False)
        h = jnp.concatenate([h, ones], axis=-1)
        out = jnp.einsum('ebh,eho->ebo', h, weight2)
        out = out.transpose(1, 0, 2)
        weighted = jnp.einsum('beo,bke->bkeo', out, topv).reshape(Bn, K * E, O)
        outputs = jnp.zeros((Bn, Sn, O), dtype=x.dtype)
        outputs = outputs.at[jnp.arange(Bn)[:, None], flat_idx].add(weighted)
        return outputs

    def _gn(v, G=32, eps=1e-05):
        B_, C_, H_, W_ = v.shape
        g = v.reshape(B_, G, C_ // G, H_, W_)
        m = jnp.mean(g, axis=(2, 3, 4), keepdims=True)
        s = jnp.var(g, axis=(2, 3, 4), keepdims=True)
        return ((g - m) / jnp.sqrt(s + eps)).reshape(v.shape)

    def _ln_c(v, eps=1e-06):
        m = jnp.mean(v, axis=1, keepdims=True)
        s = jnp.var(v, axis=1, keepdims=True)
        return (v - m) / jnp.sqrt(s + eps)

    def _ln_t(v, eps=1e-05):
        m = jnp.mean(v, axis=-1, keepdims=True)
        s = jnp.var(v, axis=-1, keepdims=True)
        return (v - m) / jnp.sqrt(s + eps)

    def _to_tokens(v):
        B_, C_, H_, W_ = v.shape
        return v.reshape(B_, C_, H_ * W_).transpose(0, 2, 1)

    def _from_tokens(t, like):
        B_, C_, H_, W_ = like.shape
        return t.transpose(0, 2, 1).reshape(B_, C_, H_, W_)
    x = x + _L0_conv_ref(_gn(x), L0_conv_w_dw, L0_conv_ln_w, L0_conv_w_off, L0_conv_wq, L0_conv_wk, L0_conv_wv, L0_conv_wo, L0_conv_rpe)
    t = _to_tokens(x)
    t = t + _L1_attn_ref(_ln_t(t))
    t = t + _L1_ffn_ref(_ln_t(t), L1_ffn_gate_w, L1_ffn_gate_b, L1_ffn_weight1, L1_ffn_weight2)
    x = _from_tokens(t, x)
    return x

_drawn_inputs = setup_inputs


def setup_inputs(seed=0):
    import zlib

    import numpy as np

    out = dict(_drawn_inputs(seed))
    spreads = {'L0_conv_ln_w': (1.0, 0.6), 'L1_ffn_gate_b': (0.0, 0.8)}
    factors = {'L0_conv_w_dw': 8.0,
     'L0_conv_w_off': 8.0,
     'L0_conv_wq': 8.0,
     'L0_conv_wk': 8.0,
     'L0_conv_wv': 8.0,
     'L0_conv_wo': 8.0,
     'L0_conv_rpe': 8.0,
     'L1_ffn_gate_w': 8.0,
     'L1_ffn_weight1': 8.0,
     'L1_ffn_weight2': 8.0}
    for name, (base, spread) in spreads.items():
        noise = np.random.default_rng([zlib.crc32(name.encode()), seed]).standard_normal(out[name].shape)
        drawn = base * np.exp(spread * noise) if base else spread * noise
        out[name] = jnp.asarray(drawn.astype(out[name].dtype))
    for name, factor in factors.items():
        out[name] = (out[name] * factor).astype(out[name].dtype)
    return out
```

```python
from contextlib import ExitStack

import numpy as np

import concourse.bass as bass
from concourse import mybir

F32 = mybir.dt.float32
U32 = mybir.dt.uint32
ALU = mybir.AluOpType
ACT = mybir.ActivationFunctionType
AX = mybir.AxisListType

P = 128
B, C = 8, 32
IMG = 16
M = IMG * IMG
NHALF = M // P
G = 2
GC = C // G
HG = 2
DH = C // (G * HG)
KS, STRIDE, PAD = 5, 4, 2
PADIMG = IMG + 2 * PAD
NK = IMG // STRIDE
N = NK * NK
RPE = 2 * IMG - 1
RPAD = RPE + 1
WIN = 24
NE, HID = 16, 128
TOPK = 8
NT = 2
B4 = B // NT
EPS = 1e-5
QK_SCALE = float(DH) ** -0.5
OFFSET = 1.0 / NK * 0.5 * (IMG - 1)
SCORE_BOUND = float(C)

CONST_COLS = {}
_n = 0
for _name, _w in (("avg", P), ("center", P), ("ident", P), ("same_b", B), ("head", HG), ("eps", 1), ("one", 1),
                  ("bound", 1), ("ref_x", 1), ("frac_x", IMG), ("steps", 16), ("signs", 5 * 16),
                  ("sample", 3 * N), ("rel_y", 4 * N), ("same_b4", NT * B)):
    CONST_COLS[_name] = (_n, _n + _w)
    _n += _w
NCONST = _n

WEIGHT_COLS = {}
_n = 0
for _name, _w in (("dw", KS * KS), ("ln_w", 1), ("w_off", 3), ("proj", 4 * G * C), ("rpe", G * HG * RPAD),
                  ("gate_w", NE), ("gate_b", 1), ("bias2", C)):
    WEIGHT_COLS[_name] = (_n, _n + _w)
    _n += _w
NWEIGHT = _n


def shape_constants():
    c = np.zeros((P, NCONST), np.float32)

    def put(name, a):
        lo, hi = CONST_COLS[name]
        c[:, lo:hi] = np.broadcast_to(np.asarray(a, np.float64).reshape(len(a), -1), (P, hi - lo))

    p = np.arange(P)
    avg = (p[:, None] // GC == p[None, :] // GC) / GC
    put("avg", avg)
    put("center", np.eye(P) - avg)
    put("ident", np.eye(P))
    put("same_b", p[:, None] // GC == np.arange(B)[None, :])
    put("head", (p[:, None] % GC) // DH == np.arange(HG)[None, :])
    put("eps", np.full((P, 1), EPS))
    put("one", np.ones((P, 1)))
    put("bound", np.full((P, 1), -SCORE_BOUND))
    ref = (np.arange(NK) + 0.5) / NK * 2 - 1
    ref_y, ref_x = np.repeat(ref, NK), np.tile(ref, NK)
    half = 0.5 * (IMG - 1)
    query = (np.arange(IMG) + 0.5) / IMG * 2 - 1
    put("ref_x", (half * (query[0] - ref_x) + IMG - 1)[p % N][:, None])
    put("frac_x", (np.arange(IMG) / IMG)[None, :] * np.ones((P, 1)))
    k = np.arange(16)
    put("steps", np.where(k == 0, 1e9, k)[None, :] * np.ones((P, 1)))
    signs = np.zeros((5, 16))
    for row, bit in enumerate((8, 4, 2, 1)):
        for j in range(bit, 16, bit):
            signs[row, j] = 1 if (j // bit) % 2 else -1
    signs[4, 1:] = 1
    put("signs", signs.reshape(1, -1) * np.ones((P, 1)))
    s = np.zeros((P, 3, N))
    for h in range(NHALF):
        s[:, h] = (p // IMG + h * (P // IMG))[:, None] - half * (ref_y + 1)[None, :]
    s[:, 2] = (p % IMG)[:, None] - half * (ref_x + 1)[None, :]
    put("sample", s)
    r = np.zeros((P, 4, N))
    for yq in range(4):
        y = 4 * (p // 32) + yq
        r[:, yq] = (half * query[y] + IMG - 1 - p % 32)[:, None] - half * ref_y[None, :]
    put("rel_y", r)
    put("same_b4", (p[:, None] // C + B4 * (np.arange(NT * B) // B)[None, :]) == (np.arange(NT * B) % B)[None, :])
    return c


def build(nc, x_in, consts_in, weights_in, w1_in, w2_in, out):
    with ExitStack() as ctx:
        def sb(name, shape, dt=F32):
            return ctx.enter_context(nc.sbuf_tensor(name, shape, dt))

        def bank(name, n=1):
            return ctx.enter_context(nc.psum_tensor(name, [P, n * 512], F32))

        def sem(name):
            return ctx.enter_context(nc.semaphore(name))

        b0123 = bank("b0123", 4)
        b01 = b0123[:, 0:1024]
        b23 = b0123[:, 1024:2048]
        b4 = bank("b4")
        b5 = bank("b5")
        b67 = bank("b67", 2)

        x_sb = sb("x_sb", [P, G, M])
        cst = sb("cst", [P, NCONST])
        wts = sb("wts", [P, NWEIGHT])
        w1_sb = sb("w1_sb", [C + 1, NE, HID])
        w2_sb = sb("w2_sb", [HID, NE, C])

        def const(name):
            lo, hi = CONST_COLS[name]
            return cst[:, lo:hi]

        def weight(name):
            lo, hi = WEIGHT_COLS[name]
            return wts[:, lo:hi]

        ident, same_b = const("ident"), const("same_b")
        proj = weight("proj").rearrange("p (w g o) -> p w g o", w=4, g=G)

        stats = sb("stats", [P, G, 6])
        meanvar = sb("meanvar", [P, G, 2])
        gn_var = sb("gn_var", [P, G])
        gn_std = sb("gn_std", [P, G])
        gn_rstd = sb("gn_rstd", [P, G])
        xn = sb("xn", [P, G, M])
        xn_tok = sb("xn_tok", [P, NHALF, G, P])
        x_tok = sb("x_tok", [P, NHALF, B, G, GC])
        wk_s = sb("wk_s", [P, G, C])
        wblk = sb("wblk", [P, 3, G, G, B, GC])
        woblk = sb("woblk", [P, G, B, C])
        gate_blk = sb("gate_blk", [P, NT, B, NE])
        q_sb = sb("q_sb", [P, G, M])
        qpad = sb("qpad", [P, G, PADIMG, PADIMG])
        taps = sb("taps", [P, G, NK, NK, KS * KS])
        off = sb("off", [P, G * N])
        off_sq = sb("off_sq", [P, G * N])
        off_var = sb("off_var", [P, G * N])
        off_std = sb("off_std", [P, G * N])
        off_rstd = sb("off_rstd", [P, G * N])
        off_w = sb("off_w", [P, G * N])
        off_n = sb("off_n", [P, G * N])
        off_act = sb("off_act", [P, G * N])
        off_blk = sb("off_blk", [P, G, B, N])
        warm = sb("warm", [P, 8])
        th = sb("th", [P, 2, G * B * N])
        thp = sb("thp", [P, 2, G * B * N])
        half_tanh = sb("half_tanh", [P, G * B * N])
        gate = sb("gate", [P, G * B * N])
        gate_m = sb("gate_m", [P, G, B, B, N])
        txh = sb("txh", [P, G])
        tx = sb("tx", [P, G])
        over = sb("over", [P, G, 16])
        signed = sb("signed", [P, G, 5, 16])
        bits = sb("bits", [P, G, 5])
        masks = sb("masks", [P, G, 5], U32)
        frac = sb("frac", [P, G])
        dist = sb("dist", [P, G, IMG])
        tap_next = sb("tap_next", [P, G, IMG])
        tap_prev = sb("tap_prev", [P, G, IMG])
        tap_nabs = sb("tap_nabs", [P, G, IMG])
        tap_here = sb("tap_here", [P, G, IMG])
        z_rel = sb("z_rel", [P, 4, G * B * N])
        a_rel = sb("a_rel", [P, 4, G * B * N])
        hat_rel = sb("hat_rel", [P, 4, G * B * N])
        z_smp = sb("z_smp", [P, 3, G * B * N])
        a_smp = sb("a_smp", [P, 3, G * B * N])
        hat_smp = sb("hat_smp", [P, 3, G * B * N])
        w_smp = sb("w_smp", [P, NHALF, G * B * N])
        xs = sb("xs", [P, G, B * N])
        kv = sb("kv", [P, HG, 2, G, B * N])
        vo = sb("vo", [P, G * HG, B * C])
        win = sb("win", [P, G, IMG * HG, WIN])
        prod = sb("prod", [P, 2, IMG, HG, IMG])
        bias = sb("bias", [P, G, HG, IMG, IMG])
        d_max = sb("d_max", [P, NHALF, 32])
        d_sub = sb("d_sub", [P, NHALF, 32, N])
        d_exp = sb("d_exp", [P, NHALF, 32, N])
        d_sum = sb("d_sum", [P, NHALF, 32])
        d_rec = sb("d_rec", [P, NHALF, 32])
        d_prob = sb("d_prob", [P, NHALF, 32, N])
        prob_t = sb("prob_t", [P, NHALF, G * HG, P])
        x1 = sb("x1", [P, NHALF * B, C])
        ln_sum = sb("ln_sum", [P, 2, NHALF * B])
        ln_mean = sb("ln_mean", [P, 2, NHALF * B])
        ln_c = sb("ln_c", [P, 2, NHALF * B, C])
        ln_sq = sb("ln_sq", [P, 2, NHALF * B, C])
        ln_ss = sb("ln_ss", [P, 2, NHALF * B])
        ln_var = sb("ln_var", [P, 2, NHALF * B])
        ln_std = sb("ln_std", [P, 2, NHALF * B])
        ln_rstd = sb("ln_rstd", [P, 2, NHALF * B])
        t1 = sb("t1", [P, NHALF * B, C])
        t1_one = sb("t1_one", [P, NHALF * B, C + 1])
        t1_t = sb("t1_t", [P, NT, M])
        e_tok = sb("e_tok", [P, B, NHALF, M])
        o_rec = sb("o_rec", [P, NHALF, B])
        o_n = sb("o_n", [P, NHALF, B, C])
        x2 = sb("x2", [P, NHALF * B, C])
        t2 = sb("t2", [P, NHALF * B, C])
        t2_t = sb("t2_t", [P, NT, M])
        g_log = sb("g_log", [P, M])
        g_max = sb("g_max", [P, 1])
        g_exp = sb("g_exp", [P, M])
        g_sum = sb("g_sum", [P, 1])
        g_rec = sb("g_rec", [P, 1])
        g_prob = sb("g_prob", [P, M])
        top = sb("top", [P, TOPK])
        rest = sb("rest", [P, M])
        picked = sb("picked", [P, M])
        picked_t = sb("picked_t", [P, NHALF, P])
        pooled = sb("pooled", [C + 1, P])
        hidden = sb("hidden", [P, NE, B])
        out2_t = sb("out2_t", [C, P])
        out2 = sb("out2", [P, C])
        out2_blk = sb("out2_blk", [P, B, C])
        y_sb = sb("y_sb", [P, NT, M])

        q_ps = b4[:, :].rearrange("p (g m) -> p g m", g=G)
        xnt_ps = b5[:, :].rearrange("p (h g c) -> p h g c", h=NHALF, g=G)
        xt_ps = b67[:, 0:512].rearrange("p (h g b c) -> p h g b c", h=NHALF, g=G, b=B)
        cen_ps = b67[:, 512:544]
        var_ps = b67[:, 544:576]
        tx_ps = b67[:, 576:578]
        off_ps = b01[:, 0:3 * G * B * N].rearrange("p (j n) -> p j n", j=3)
        row_ps = b0123[:, :].rearrange("p (yb g r c) -> p yb g r c", yb=4, g=G, c=RPAD)
        xs_ps = b4[:, 0:G * P].rearrange("p (g n) -> p g n", g=G)
        kv_ps = b5[:, :].rearrange("p (w g n) -> p w g n", w=2, g=G)
        vo_ps = [t[:, 256 * j:256 * j + 256] for t in (b4, b5) for j in range(2)]
        lg_ps = b67[:, :].rearrange("p (h k j) -> p h k j", h=NHALF, k=G * HG)
        pt_ps = b01.rearrange("p (h k m) -> p h k m", h=NHALF, m=P)
        att_ps = b23.rearrange("p (h j) -> p h j", h=NHALF)[:, :, 0:B * C]
        t1t_ps = b01[:, 0:512].rearrange("p (t m) -> p t m", t=NT)
        o_ps = b01.rearrange("p (h k) -> p h k", h=NHALF)[:, :, 0:B * (C + 1)] \
            .rearrange("p h (b c) -> p h b c", b=B)
        t2t_ps = b23[:, 0:512].rearrange("p (t m) -> p t m", t=NT)
        g_ps = b23[:, 512:768]
        pickt_ps = b4[:, 0:256].rearrange("p (h k) -> p h k", h=NHALF)
        pool_ps = b5[0:C, 0:P]
        hid_ps = b67[:, 0:P].rearrange("p (e b) -> p e b", e=NE)
        out2t_ps = b67[0:C, 512:512 + P].rearrange("p (b e) -> p e b", e=NE)
        out2_ps = b4[:, 256:256 + C]
        y_ps = b01.rearrange("p (t m) -> p t m", t=NT)[:, :, 0:M]

        x_loaded = [sem(f"x_loaded{g}") for g in range(G)]
        const_loaded = sem("const_loaded")
        weights_loaded = sem("weights_loaded")
        w1_loaded, w2_loaded = sem("w1_loaded"), sem("w2_loaded")
        stored = sem("stored")
        dve_step = sem("dve_step")
        pool_step = sem("pool_step")
        act_step = sem("act_step")
        gn_var_ready, gn_std_ready, xn_ready = sem("gn_var_ready"), sem("gn_std_ready"), sem("xn_ready")
        wq_ready, wkvo_ready, gate_blk_ready = sem("wq_ready"), sem("wkvo_ready"), sem("gate_blk_ready")
        qpad_zeroed, t1_one_ready = sem("qpad_zeroed"), sem("t1_one_ready")
        pooled_one_set = sem("pooled_one_set")
        q_done, q_copied = sem("q_done"), sem("q_copied")
        turned, xn_tok_copied, x_tok_copied = sem("turned"), sem("xn_tok_copied"), sem("x_tok_copied")
        taps_ready, off_ready = sem("taps_ready"), sem("off_ready")
        centered, squared, var_done, off_var_ready = sem("centered"), sem("squared"), sem("var_done"), sem("off_var_ready")
        off_std_ready, off_n_ready, off_act_ready = sem("off_std_ready"), sem("off_n_ready"), sem("off_act_ready")
        off_blk_ready, off_done = sem("off_blk_ready"), sem("off_done")
        tanh_ready, txh_ready, half_tanh_ready = sem("tanh_ready"), sem("txh_ready"), sem("half_tanh_ready")
        thp_ready, z_smp_ready, hat_smp_ready = sem("thp_ready"), sem("z_smp_ready"), sem("hat_smp_ready")
        w_smp_ready, gate_m_ready = sem("w_smp_ready"), sem("gate_m_ready")
        z_rel_ready, hat_rel_ready = sem("z_rel_ready"), sem("hat_rel_ready")
        sampled, xs_ready, kv_done, kv_ready = sem("sampled"), sem("xs_ready"), sem("kv_done"), sem("kv_ready")
        vo_done, vo_copied = sem("vo_done"), sem("vo_copied")
        rows_done, win_copied, rows_used = sem("rows_done"), sem("win_copied"), sem("rows_used")
        bias_ready, logits_done, d_sub_ready = sem("bias_ready"), sem("logits_done"), sem("d_sub_ready")
        d_exp_ready, d_prob_ready = sem("d_exp_ready"), sem("d_prob_ready")
        prob_turned, prob_copied, att_done = sem("prob_turned"), sem("prob_copied"), sem("att_done")
        ln_c_ready, ln_sq_ready, ln_var_ready, ln_std_ready = (
            sem("ln_c_ready"), sem("ln_sq_ready"), sem("ln_var_ready"), sem("ln_std_ready"))
        t1_ready, t1_turned, t1_copied = sem("t1_ready"), sem("t1_turned"), sem("t1_copied")
        scores_done, exp_ready, o_done, x2_ready = sem("scores_done"), sem("exp_ready"), sem("o_done"), sem("x2_ready")
        t2_ready, t2_turned, t2_copied, g_done = sem("t2_ready"), sem("t2_turned"), sem("t2_copied"), sem("g_done")
        g_max_ready, g_exp_ready = sem("g_max_ready"), sem("g_exp_ready")
        picked_ready, picked_turned, picked_copied = sem("picked_ready"), sem("picked_turned"), sem("picked_copied")
        pooled_done, pooled_ready, hidden_done, hidden_ready = (
            sem("pooled_done"), sem("pooled_ready"), sem("hidden_done"), sem("hidden_ready"))
        out2t_done, out2t_copied, out2_done, out2_ready = (
            sem("out2t_done"), sem("out2t_copied"), sem("out2_done"), sem("out2_ready"))
        y_done, y_ready = sem("y_done"), sem("y_ready")


        def conv_view(g, i):
            rows = qpad[:, g, STRIDE * i:STRIDE * i + KS, :]
            return bass.AP(tensor=rows.tensor, offset=rows.offset,
                           ap=[list(rows.ap[0]), [STRIDE, NK], [PADIMG, KS], [1, KS]])

        score_parts = [(0, 2, b23), (2, 1, b4[:, :]), (3, 1, b5[:, :]), (4, 2, b67[:, :]), (6, 2, b23)]

        block = ctx.enter_context(nc.Block())

        @block.sync
        def _(sp):
            for g in range(G):
                sp.dma_start(x_sb[:, g, :], x_in[g]).then_inc(x_loaded[g], 16)
            sp.dma_start(wts[:, :], weights_in).then_inc(weights_loaded, 16)
            sp.dma_start(w1_sb[:, :, :], w1_in.rearrange("e d h -> d e h")).then_inc(w1_loaded, 16)
            sp.wait_ge(y_ready, 1)
            sp.dma_start(out[0], y_sb[:, 0, :]).then_inc(stored, 16)
            sp.wait_ge(stored, 32)

        @block.gpsimd
        def _(pool):
            steps = [0]

            def link(ins):
                steps[0] += 1
                ins.then_inc(pool_step, 1)
                pool.wait_ge(pool_step, steps[0])

            nc.gpsimd.memset(qpad[:, :, :, :], 0.0).then_inc(qpad_zeroed, 1)
            nc.gpsimd.memset(t1_one[:, :, C:C + 1], 1.0).then_inc(t1_one_ready, 1)
            pool.wait_ge(weights_loaded, 16)
            pool.wait_ge(const_loaded, 16)

            def blocks(dst, src, n_groups, width):
                return nc.gpsimd.tensor_tensor(
                    dst, src.unsqueeze(2).to_broadcast([P, n_groups, B, width]),
                    same_b.unsqueeze(1).unsqueeze(3).to_broadcast([P, n_groups, B, width]), ALU.mult)

            link(nc.gpsimd.tensor_scalar(wk_s[:, :, :], proj[:, 1], QK_SCALE, None, ALU.mult))
            for g in range(G):
                blocks(wblk[:, 1, g], wk_s[:, g].rearrange("p (g o) -> p g o", g=G), G, GC).then_inc(wkvo_ready, 1)
                blocks(wblk[:, 2, g], proj[:, 2, g].rearrange("p (g o) -> p g o", g=G), G, GC).then_inc(wkvo_ready, 1)
            pool.wait_ge(q_copied, 1)
            dw = weight("dw").rearrange("p (a b) -> p a b", a=KS).unsqueeze(1).to_broadcast([P, NK, KS, KS])
            for i in range(NK):
                nc.gpsimd.tensor_tensor(taps[:, 1, i].rearrange("p j (a b) -> p j a b", a=KS), conv_view(1, i), dw,
                                        ALU.mult).then_inc(taps_ready, 1)
            for g in range(G):
                blocks(woblk[:, g].unsqueeze(1), proj[:, 3, g].unsqueeze(1), 1, C).then_inc(wkvo_ready, 1)
            same_b4 = const("same_b4").rearrange("p (t b) -> p t b", t=NT)
            nc.gpsimd.tensor_tensor(
                gate_blk[:, :, :, :],
                weight("gate_w").unsqueeze(1).unsqueeze(1).to_broadcast([P, NT, B, NE]),
                same_b4.unsqueeze(3).to_broadcast([P, NT, B, NE]), ALU.mult).then_inc(gate_blk_ready, 1)
            pool.wait_ge(thp_ready, 1)
            smp = const("sample").rearrange("p (k n) -> p k n", k=3)

            def grid(a):
                return a.rearrange("p (q n) -> p q n", n=N)

            for k in range(3):
                nc.gpsimd.tensor_tensor(
                    grid(z_smp[:, k]), grid(thp[:, 0 if k < NHALF else 1]),
                    smp[:, k].unsqueeze(1).to_broadcast([P, G * B, N]), ALU.add).then_inc(z_smp_ready, 1)
            pool.wait_ge(half_tanh_ready, 1)
            link(nc.gpsimd.tensor_scalar(gate[:, :], half_tanh[:, :], 0.5, 0.5, ALU.mult, ALU.add))
            pool.wait_ge(hat_smp_ready, 1)
            for h in range(NHALF):
                nc.gpsimd.tensor_tensor(w_smp[:, h], hat_smp[:, h], hat_smp[:, 2], ALU.mult).then_inc(w_smp_ready, 1)
            for g in range(G):
                nc.gpsimd.tensor_tensor(
                    gate_m[:, g, 0], gate[:, :].rearrange("p (g b n) -> p g b n", g=G, b=B)[:, g],
                    same_b.unsqueeze(2).to_broadcast([P, B, N]), ALU.mult).then_inc(gate_m_ready, 1)
            pool.wait_ge(ln_c_ready, 1)
            nc.gpsimd.tensor_tensor(ln_sq[:, 0], ln_c[:, 0], ln_c[:, 0], ALU.mult).then_inc(ln_sq_ready, 1)
            pool.wait_ge(t1_ready, 1)
            nc.gpsimd.tensor_copy(t1_one[:, :, 0:C], t1[:, :, :]).then_inc(t1_one_ready, 1)
            pool.wait_ge(ln_c_ready, 2)
            nc.gpsimd.tensor_tensor(ln_sq[:, 1], ln_c[:, 1], ln_c[:, 1], ALU.mult).then_inc(ln_sq_ready, 1)

        @block.scalar
        def _(act):
            act.dma_start(cst[:, :], consts_in).then_inc(const_loaded, 16)
            act.dma_start(w2_sb[:, :, :], w2_in[:, 0:HID, :].rearrange("e h o -> h e o")).then_inc(w2_loaded, 16)
            act.wait_ge(const_loaded, 16)
            nc.scalar.activation(warm[:, 0:1], const("one"), ACT.Sqrt)
            act.wait_ge(gn_var_ready, 1)
            nc.scalar.activation(gn_std[:, :], gn_var[:, :], ACT.Sqrt).then_inc(gn_std_ready, 1)
            act.wait_ge(q_done, 1)
            act.wait_ge(qpad_zeroed, 1)
            nc.scalar.activation(qpad[:, :, PAD:PAD + IMG, PAD:PAD + IMG],
                                 q_ps.rearrange("p g (y x) -> p g y x", y=IMG), ACT.Copy).then_inc(q_copied, 1)
            nc.scalar.activation(q_sb[:, :, :], q_ps, ACT.Copy).then_inc(q_copied, 1)
            act.wait_ge(turned, 1)
            nc.scalar.activation(xn_tok[:, :, :, :], xnt_ps, ACT.Copy).then_inc(xn_tok_copied, 1)
            act.wait_ge(turned, 2)
            for h in range(NHALF):
                nc.scalar.activation(x_tok[:, h].rearrange("p b g c -> p g b c"), xt_ps[:, h],
                                     ACT.Copy).then_inc(x_tok_copied, 1)
            act.wait_ge(centered, 1)
            nc.scalar.activation(off_sq[:, :], cen_ps, ACT.Square).then_inc(squared, 1)
            act.wait_ge(off_var_ready, 1)
            nc.scalar.activation(off_std[:, :], off_var[:, :], ACT.Sqrt).then_inc(off_std_ready, 1)
            nc.scalar.activation(warm[:, 1:2], const("one"), ACT.Gelu)
            act.wait_ge(off_n_ready, 1)
            nc.scalar.activation(off_act[:, :], off_n[:, :], ACT.Gelu).then_inc(off_act_ready, 1)
            act.wait_ge(off_done, 1)
            nc.scalar.activation(th[:, :, :], off_ps[:, 0:2], ACT.Tanh).then_inc(tanh_ready, 1)
            nc.scalar.activation(txh[:, :], tx_ps, ACT.Tanh).then_inc(txh_ready, 1)
            nc.scalar.activation(half_tanh[:, :], off_ps[:, 2], ACT.Tanh, scale=0.5).then_inc(half_tanh_ready, 1)
            act.wait_ge(z_smp_ready, 3)
            nc.scalar.activation(a_smp[:, :, :], z_smp[:, :, :], ACT.Abs).then_inc(act_step, 1)
            act.wait_ge(act_step, 1)
            nc.scalar.activation(hat_smp[:, :, :], a_smp[:, :, :], ACT.Relu, bias=const("one"),
                                 scale=-1.0).then_inc(hat_smp_ready, 1)
            act.wait_ge(z_rel_ready, 1)
            nc.scalar.activation(a_rel[:, :, :], z_rel[:, :, :], ACT.Abs).then_inc(act_step, 1)
            act.wait_ge(act_step, 2)
            nc.scalar.activation(hat_rel[:, :, :], a_rel[:, :, :], ACT.Relu, bias=const("one"),
                                 scale=-1.0).then_inc(hat_rel_ready, 1)
            nc.scalar.activation(warm[:, 2:3], const("one"), ACT.Exp)
            act.wait_ge(rows_done, 1)
            for g in range(G):
                nc.scalar.activation(win[:, g].rearrange("p (k r) c -> p k r c", k=4), row_ps[:, :, g, :, 0:WIN],
                                     ACT.Copy).then_inc(win_copied, 1)
            act.wait_ge(vo_done, 1)
            for j in range(2):
                nc.scalar.activation(vo[:, 2 * j:2 * j + 2, :].rearrange("p a b -> p (a b)"), (b4, b5)[j][:, :],
                                     ACT.Copy).then_inc(vo_copied, 1)
            for h in range(NHALF):
                act.wait_ge(d_sub_ready, h + 1)
                nc.scalar.activation(d_exp[:, h], d_sub[:, h], ACT.Exp).then_inc(d_exp_ready, 1)
            for h in range(NHALF):
                act.wait_ge(prob_turned, h + 1)
                nc.scalar.activation(prob_t[:, h], pt_ps[:, h],
                                     ACT.Copy).then_inc(prob_copied, 1)
            nc.scalar.activation(warm[:, 3:4], const("one"), ACT.Sqrt)
            act.wait_ge(ln_var_ready, 1)
            nc.scalar.activation(ln_std[:, 0], ln_var[:, 0], ACT.Sqrt).then_inc(ln_std_ready, 1)
            nc.scalar.activation(warm[:, 4:5], const("one"), ACT.Exp)
            act.wait_ge(t1_turned, 1)
            nc.scalar.activation(t1_t[:, :, :], t1t_ps, ACT.Copy).then_inc(t1_copied, 1)
            for n, (b0, nb, ps) in enumerate(score_parts):
                act.wait_ge(scores_done, n + 1)
                nc.scalar.activation(e_tok[:, b0:b0 + nb].rearrange("p b h q -> p (b h q)"), ps, ACT.Exp,
                                     bias=const("bound")).then_inc(exp_ready, 1)
            nc.scalar.activation(warm[:, 5:6], const("one"), ACT.Sqrt)
            act.wait_ge(ln_var_ready, 2)
            nc.scalar.activation(ln_std[:, 1], ln_var[:, 1], ACT.Sqrt).then_inc(ln_std_ready, 1)
            nc.scalar.activation(warm[:, 6:7], const("one"), ACT.Exp)
            act.wait_ge(t2_turned, 1)
            nc.scalar.activation(t2_t[:, :, :], t2t_ps, ACT.Copy).then_inc(t2_copied, 1)
            act.wait_ge(g_max_ready, 1)
            nc.scalar.activation(g_exp[:, :], g_log[:, :], ACT.Exp, bias=g_max[:, 0:1],
                                 accum_out=g_sum[:, 0:1]).then_inc(g_exp_ready, 1)
            nc.scalar.activation(warm[:, 7:8], const("one"), ACT.Gelu)
            act.wait_ge(hidden_done, 1)
            nc.scalar.activation(hidden[:, :, :], hid_ps, ACT.Gelu).then_inc(hidden_ready, 1)
            act.wait_ge(y_done, 1)
            nc.scalar.activation(y_sb[:, 1, :], y_ps[:, 1], ACT.Copy).then_inc(act_step, 1)
            act.wait_ge(act_step, 3)
            act.dma_start(out[1], y_sb[:, 1, :]).then_inc(stored, 16)

        @block.tensor
        def _(pe):
            mm = nc.tensor.matmul

            pe.wait_ge(wq_ready, 2)
            pe.wait_ge(xn_ready, 2)
            for g in range(G):
                for gi in range(G):
                    last = mm(q_ps[:, g], wblk[:, 0, gi, g].rearrange("p b o -> p (b o)"), xn[:, gi],
                              start=(gi == 0), stop=(gi == G - 1))
            last.then_inc(q_done, 1)
            pe.wait_ge(const_loaded, 16)
            for h in range(NHALF):
                for g in range(G):
                    last = nc.tensor.transpose(xnt_ps[:, h, g], xn[:, g, h * P:(h + 1) * P], ident)
            last.then_inc(turned, 1)
            for h in range(NHALF):
                for g in range(G):
                    last = nc.tensor.transpose(xt_ps[:, h, g].rearrange("p b c -> p (b c)"),
                                               x_sb[:, g, h * P:(h + 1) * P], ident)
            last.then_inc(turned, 1)
            pe.wait_ge(off_ready, 1)
            mm(cen_ps, const("center"), off[:, :], start=True, stop=True).then_inc(centered, 1)
            pe.wait_ge(squared, 1)
            mm(var_ps, const("avg"), off_sq[:, :], start=True, stop=True).then_inc(var_done, 1)
            pe.wait_ge(off_blk_ready, 1)
            cols = off_blk[:, :, :, :].rearrange("p g b n -> p (g b n)")
            for j in range(3):
                mm(off_ps[:, j], weight("w_off")[:, j:j + 1].to_broadcast([P, P]), cols, start=True, stop=True)
            for g in range(G):
                last = mm(tx_ps[:, g:g + 1], off_blk[:, g].rearrange("p b n -> p (b n)"),
                          weight("w_off")[:, 1:2], start=True, stop=True)
            last.then_inc(off_done, 1)
            pe.wait_ge(w_smp_ready, 2)
            pe.wait_ge(xn_tok_copied, 1)
            pe.wait_ge(q_copied, 2)
            for g in range(G):
                for h in range(NHALF):
                    last = mm(xs_ps[:, g], xn_tok[:, h, g], w_smp[:, h, g * P:(g + 1) * P],
                              start=(h == 0), stop=(h == NHALF - 1))
            last.then_inc(sampled, 1)
            pe.wait_ge(hat_rel_ready, 1)
            pe.wait_ge(half_tanh_ready, 1)
            rpe = weight("rpe").rearrange("p (g k) -> p g k", g=G)
            for g in range(G):
                for yq in range(4):
                    for yb in range(4):
                        rows = slice(32 * yb, 32 * yb + 32)
                        last = mm(row_ps[:, yb, g, HG * yq:HG * yq + HG].rearrange("p r c -> p (r c)"), hat_rel[rows, yq, g * P:(g + 1) * P], rpe[rows, g],
                                  start=True, stop=True)
            last.then_inc(rows_done, 1)
            pe.wait_ge(xs_ready, 1)
            pe.wait_ge(wkvo_ready, 6)
            for w in range(2):
                for g in range(G):
                    for gi in range(G):
                        last = mm(kv_ps[:, w, g], wblk[:, 1 + w, gi, g].rearrange("p b o -> p (b o)"), xs[:, gi],
                                  start=(gi == 0), stop=(gi == G - 1))
            last.then_inc(kv_done, 1)
            pe.wait_ge(kv_ready, HG)
            for g in range(G):
                for hh in range(HG):
                    last = mm(vo_ps[g * HG + hh], kv[:, hh, 1, g], woblk[:, g].rearrange("p b o -> p (b o)"),
                              start=True, stop=True)
            last.then_inc(vo_done, 1)
            pe.wait_ge(x_tok_copied, 2)
            pe.wait_ge(txh_ready, 1)
            pe.wait_ge(q_copied, 2)
            for h in range(NHALF):
                for g in range(G):
                    for hh in range(HG):
                        mm(lg_ps[:, h, g * HG + hh], q_sb[:, g, h * P:(h + 1) * P], kv[:, hh, 0, g], start=(g + hh == 0), stop=False,
                           skip_group_check=True)
            pe.wait_ge(bias_ready, G)
            for h in range(NHALF):
                for g in range(G):
                    for hh in range(HG):
                        last = mm(lg_ps[:, h, g * HG + hh],
                                  bias[:, g, hh, 8 * h:8 * h + 8].rearrange("p y x -> p (y x)"), ident,
                                  start=False, stop=True, skip_group_check=True)
                last.then_inc(logits_done, 1)
            pe.wait_ge(rows_used, G)
            for h in range(NHALF):
                pe.wait_ge(d_prob_ready, h + 1)
                for k in range(G * HG):
                    last = nc.tensor.transpose(
                        pt_ps[:, h, k],
                        d_prob[:, h, 8 * k:8 * k + 8].rearrange("p b n -> p (b n)"), ident)
                last.then_inc(prob_turned, 1)
            pe.wait_ge(vo_copied, 2)
            pe.wait_ge(rows_used, 2)
            for h in range(NHALF):
                pe.wait_ge(prob_copied, h + 1)
                for k in range(G * HG):
                    last = mm(att_ps[:, h], prob_t[:, h, k], vo[:, k],
                              start=(k == 0), stop=(k == G * HG - 1))
                last.then_inc(att_done, 1)
            pe.wait_ge(t1_ready, 1)
            t1_rows = t1[:, :, :].rearrange("p (h b) c -> p h (b c)", h=NHALF)
            for t in range(NT):
                for h in range(NHALF):
                    last = nc.tensor.transpose(t1t_ps[:, t, h * P:(h + 1) * P],
                                               t1_rows[:, h, P * t:P * t + P], ident)
            last.then_inc(t1_turned, 1)
            pe.wait_ge(t1_copied, 1)
            pe.wait_ge(t1_one_ready, 2)

            def scores(n):
                b0, nb, ps = score_parts[n]
                for j in range(nb):
                    b = b0 + j
                    rows = slice(C * (b % B4), C * (b % B4) + C)
                    for h in range(NHALF):
                        last = mm(ps[:, 512 * j + M * h:512 * j + M * h + M],
                                  t1_t[rows, b // B4, h * P:(h + 1) * P], t1_t[rows, b // B4, :],
                                  start=True, stop=True)
                last.then_inc(scores_done, 1)

            def attend(n):
                b0, nb, _ = score_parts[n]
                pe.wait_ge(exp_ready, n + 1)
                for b in range(b0, b0 + nb):
                    for hq in range(NHALF):
                        for hk in range(NHALF):
                            last = mm(o_ps[:, hq, b], e_tok[:, b, hk, hq * P:(hq + 1) * P], t1_one[:, hk * B + b],
                                      start=(hk == 0), stop=(hk == NHALF - 1))
                if n == len(score_parts) - 1:
                    last.then_inc(o_done, 1)

            for n in range(4):
                scores(n)
            attend(0)
            scores(4)
            for n in range(1, 5):
                attend(n)
            pe.wait_ge(t2_ready, 1)
            t2_rows = t2[:, :, :].rearrange("p (h b) c -> p h (b c)", h=NHALF)
            for t in range(NT):
                for h in range(NHALF):
                    last = nc.tensor.transpose(t2t_ps[:, t, h * P:(h + 1) * P], t2_rows[:, h, P * t:P * t + P], ident)
            last.then_inc(t2_turned, 1)
            x2_rows = x2[:, :, :].rearrange("p (h b) c -> p h (b c)", h=NHALF)
            for t in range(NT):
                for h in range(NHALF):
                    mm(y_ps[:, t, h * P:(h + 1) * P], x2_rows[:, h, P * t:P * t + P], ident,
                       start=(h == 0), stop=False, skip_group_check=True)
            pe.wait_ge(t2_copied, 1)
            pe.wait_ge(gate_blk_ready, 1)
            for t in range(NT):
                last = mm(g_ps, gate_blk[:, t].rearrange("p b e -> p (b e)"), t2_t[:, t],
                          start=(t == 0), stop=(t == NT - 1))
            last.then_inc(g_done, 1)
            pe.wait_ge(picked_ready, 1)
            for h in range(NHALF):
                last = nc.tensor.transpose(pickt_ps[:, h], picked[:, h * P:(h + 1) * P], ident)
            last.then_inc(picked_turned, 1)
            pe.wait_ge(picked_copied, 1)
            for b in range(B):
                for h in range(NHALF):
                    last = mm(pool_ps[:, NE * b:NE * b + NE], t2[:, h * B + b, :], picked_t[:, h, NE * b:NE * b + NE],
                              start=(h == 0), stop=(h == NHALF - 1))
            last.then_inc(pooled_done, 1)
            pe.wait_ge(pooled_ready, 1)
            pe.wait_ge(pooled_one_set, 1)
            pe.wait_ge(w1_loaded, 16)
            for e in range(NE):
                last = mm(hid_ps[:, e], w1_sb[:, e, :],
                          pooled[:, :].rearrange("p (b e) -> p e b", e=NE)[:, e], start=True, stop=True)
            last.then_inc(hidden_done, 1)
            pe.wait_ge(hidden_ready, 1)
            pe.wait_ge(w2_loaded, 16)
            for e in range(NE):
                last = mm(out2t_ps[:, e], w2_sb[:, e, :], hidden[:, e, :], start=True, stop=True)
            last.then_inc(out2t_done, 1)
            pe.wait_ge(out2t_copied, 1)
            nc.tensor.transpose(out2_ps, out2_t[:, :], ident[0:C, 0:C]).then_inc(out2_done, 1)
            pe.wait_ge(out2_ready, 1)
            for t in range(NT):
                last = mm(y_ps[:, t], out2_blk[:, B4 * t:B4 * t + B4].rearrange("p b o -> p (b o)"), picked[:, :],
                          start=False, stop=True, skip_group_check=True)
            last.then_inc(y_done, 1)

        @block.vector
        def _(dve):
            steps = [0]

            def link(ins):
                steps[0] += 1
                ins.then_inc(dve_step, 1)
                dve.wait_ge(dve_step, steps[0])

            tt = nc.vector.tensor_tensor
            ts = nc.vector.tensor_scalar

            nc.vector.memset(pooled[C:C + 1, :], 1.0).then_inc(pooled_one_set, 1)
            for g in range(G):
                dve.wait_ge(x_loaded[g], 16)
                link(nc.vector.bn_stats(stats[:, g], x_sb[:, g]))
            for g in range(G):
                last = nc.vector.bn_aggr(meanvar[:, g], stats[:, g])
            link(last)
            ts(gn_var[:, :], meanvar[:, :, 1], EPS, None, ALU.add).then_inc(gn_var_ready, 1)
            dve.wait_ge(weights_loaded, 16)
            dve.wait_ge(const_loaded, 16)
            for gi in range(G):
                tt(wblk[:, 0, gi],
                   proj[:, 0, gi].rearrange("p (g o) -> p g o", g=G).unsqueeze(2).to_broadcast([P, G, B, GC]),
                   same_b.unsqueeze(1).unsqueeze(3).to_broadcast([P, G, B, GC]), ALU.mult).then_inc(wq_ready, 1)
            dve.wait_ge(gn_std_ready, 1)
            link(nc.vector.reciprocal(gn_rstd[:, :], gn_std[:, :]))
            for g in range(G):
                ts(xn[:, g], x_sb[:, g], meanvar[:, g, 0:1], gn_rstd[:, g:g + 1], ALU.subtract,
                   ALU.mult).then_inc(xn_ready, 1)
            dve.wait_ge(q_copied, 1)
            dw = weight("dw").rearrange("p (a b) -> p a b", a=KS).unsqueeze(1).to_broadcast([P, NK, KS, KS])
            for i in range(NK):
                last = tt(taps[:, 0, i].rearrange("p j (a b) -> p j a b", a=KS), conv_view(0, i), dw, ALU.mult)
            link(last)
            nc.vector.tensor_reduce(off[:, 0:N], taps[:, 0].rearrange("p i j k -> p (i j) k"), AX.X, ALU.add)
            dve.wait_ge(taps_ready, NK)
            nc.vector.tensor_reduce(off[:, N:2 * N], taps[:, 1].rearrange("p i j k -> p (i j) k"), AX.X,
                                    ALU.add).then_inc(off_ready, 1)
            dve.wait_ge(off_ready, 1)
            link(ts(off_w[:, :], off[:, :], weight("ln_w"), None, ALU.mult))
            dve.wait_ge(var_done, 1)
            ts(off_var[:, :], var_ps, EPS, None, ALU.add).then_inc(off_var_ready, 1)
            dve.wait_ge(off_std_ready, 1)
            link(nc.vector.reciprocal(off_rstd[:, :], off_std[:, :]))
            tt(off_n[:, :], off_w[:, :], off_rstd[:, :], ALU.mult).then_inc(off_n_ready, 1)
            dve.wait_ge(off_act_ready, 1)
            tt(off_blk[:, :, :, :],
               off_act[:, :].rearrange("p (g n) -> p g n", g=G).unsqueeze(2).to_broadcast([P, G, B, N]),
               same_b.unsqueeze(1).unsqueeze(3).to_broadcast([P, G, B, N]), ALU.mult).then_inc(off_blk_ready, 1)
            dve.wait_ge(tanh_ready, 1)
            ts(thp[:, :, :], th[:, :, :], -OFFSET, None, ALU.mult).then_inc(thp_ready, 1)
            dve.wait_ge(thp_ready, 1)
            rel = const("rel_y").rearrange("p (k n) -> p k n", k=4)
            tt(z_rel[:, :, :].rearrange("p k (q n) -> p k q n", n=N),
               thp[:, 0].rearrange("p (q n) -> p q n", n=N).unsqueeze(1).to_broadcast([P, 4, G * B, N]),
               rel.unsqueeze(2).to_broadcast([P, 4, G * B, N]), ALU.add).then_inc(z_rel_ready, 1)
            dve.wait_ge(txh_ready, 1)
            link(ts(tx[:, :], txh[:, :], -OFFSET, const("ref_x"), ALU.mult, ALU.add))
            link(tt(over[:, :, :], tx[:, :].unsqueeze(2).to_broadcast([P, G, 16]),
                    const("steps").unsqueeze(1).to_broadcast([P, G, 16]), ALU.is_ge))
            link(tt(signed[:, :, :, :], over[:, :, :].unsqueeze(2).to_broadcast([P, G, 5, 16]),
                    const("signs").rearrange("p (k j) -> p k j", k=5).unsqueeze(1).to_broadcast([P, G, 5, 16]),
                    ALU.mult))
            link(nc.vector.tensor_reduce(bits[:, :, :], signed[:, :, :, :], AX.X, ALU.add))
            nc.vector.tensor_copy(masks[:, :, :], bits[:, :, :])
            link(tt(frac[:, :], tx[:, :], bits[:, :, 4], ALU.subtract))
            link(tt(dist[:, :, :], frac[:, :].unsqueeze(2).to_broadcast([P, G, IMG]),
                    const("frac_x").unsqueeze(1).to_broadcast([P, G, IMG]), ALU.subtract))
            ts(tap_next[:, :, :], dist[:, :, :], 0.0, None, ALU.max)
            ts(tap_prev[:, :, :], dist[:, :, :], -1.0, 0.0, ALU.mult, ALU.max)
            link(nc.vector.scalar_tensor_tensor(out=tap_nabs[:, :, :], in0=dist[:, :, :], scalar=-1.0,
                                                in1=dist[:, :, :], op0=ALU.mult, op1=ALU.min))
            link(ts(tap_here[:, :, :], tap_nabs[:, :, :], 1.0, None, ALU.add))
            dve.wait_ge(sampled, 1)
            dve.wait_ge(gate_m_ready, G)
            tt(xs[:, :, :], xs_ps, gate_m[:, :, 0].rearrange("p g b n -> p g (b n)"), ALU.mult).then_inc(xs_ready, 1)
            dve.wait_ge(kv_done, 1)
            for hh in range(HG):
                ts(kv[:, hh].rearrange("p w g n -> p (w g n)"), b5[:, :], const("head")[:, hh:hh + 1], None,
                   ALU.mult).then_inc(kv_ready, 1)
            for g in range(G):
                dve.wait_ge(win_copied, G)

                def shifted(width, data, bit):
                    return nc.vector.copy_predicated(
                        win[:, g, :, 0:width], masks[:, g, bit:bit + 1].unsqueeze(2).to_broadcast(
                            [P, IMG * HG, width]), data)

                nc.vector.copy_predicated(
                    win[:, g].rearrange("p (k r) c -> p k r c", k=4),
                    masks[:, g, 0:1].unsqueeze(2).unsqueeze(3).to_broadcast([P, 4, 2 * 4, WIN]),
                    row_ps[:, :, g, :, 8:32]).then_inc(rows_used, 1)
                dve.wait_ge(rows_used, g + 1)
                link(shifted(20, win[:, g, :, 4:24], 1))
                link(shifted(18, win[:, g, :, 2:20], 2))
                link(shifted(17, win[:, g, :, 1:18], 3))
                w4 = win[:, g].rearrange("p (y h) c -> p y h c", h=HG)

                def col(w, n):
                    return w.unsqueeze(1).unsqueeze(1).to_broadcast([P, IMG, HG, n])

                out_g = bias[:, g].rearrange("p h y x -> p y h x")
                tt(out_g, w4[:, :, :, 0:16], col(tap_here[:, g], IMG), ALU.mult)
                link(tt(prod[:, 0], w4[:, :, :, 1:17], col(tap_next[:, g], IMG), ALU.mult))
                tt(prod[:, 1, :, :, 0:15], w4[:, :, :, 0:15], col(tap_prev[:, g, 1:16], IMG - 1), ALU.mult)
                link(tt(out_g, out_g, prod[:, 0], ALU.add))
                tt(out_g[:, :, :, 1:16], out_g[:, :, :, 1:16], prod[:, 1, :, :, 0:15], ALU.add).then_inc(bias_ready, 1)
            dve.wait_ge(bias_ready, G)
            lg_rows = [lg_ps[:, h].rearrange("p k (b n) -> p (k b) n", n=N) for h in range(NHALF)]
            for h in range(NHALF):
                dve.wait_ge(logits_done, h + 1)
                link(nc.vector.tensor_reduce(d_max[:, h], lg_rows[h], AX.X, ALU.max))
                tt(d_sub[:, h], lg_rows[h], d_max[:, h].unsqueeze(2).to_broadcast([P, 32, N]),
                   ALU.subtract).then_inc(d_sub_ready, 1)
            for h in range(NHALF):
                dve.wait_ge(d_exp_ready, h + 1)
                link(nc.vector.tensor_reduce(d_sum[:, h], d_exp[:, h], AX.X, ALU.add))
                link(nc.vector.reciprocal(d_rec[:, h], d_sum[:, h]))
                tt(d_prob[:, h], d_exp[:, h], d_rec[:, h].unsqueeze(2).to_broadcast([P, 32, N]),
                   ALU.mult).then_inc(d_prob_ready, 1)
            x_rows = x_tok[:, :, :, :, :].rearrange("p h b g c -> p h (b g c)")
            for h in range(NHALF):
                dve.wait_ge(att_done, h + 1)
                link(tt(x1[:, h * B:(h + 1) * B, :].rearrange("p b c -> p (b c)"), att_ps[:, h], x_rows[:, h], ALU.add))

            def layernorm(k, src, dst):
                link(nc.vector.tensor_reduce(ln_sum[:, k], src, AX.X, ALU.add))
                link(ts(ln_mean[:, k], ln_sum[:, k], 1.0 / C, None, ALU.mult))
                tt(ln_c[:, k], src, ln_mean[:, k].unsqueeze(2).to_broadcast([P, NHALF * B, C]),
                   ALU.subtract).then_inc(ln_c_ready, 1)
                dve.wait_ge(ln_sq_ready, k + 1)
                link(nc.vector.tensor_reduce(ln_ss[:, k], ln_sq[:, k], AX.X, ALU.add))
                ts(ln_var[:, k], ln_ss[:, k], 1.0 / C, EPS, ALU.mult, ALU.add).then_inc(ln_var_ready, 1)
                dve.wait_ge(ln_std_ready, k + 1)
                dve.wait_ge(ln_c_ready, k + 1)
                link(nc.vector.reciprocal(ln_rstd[:, k], ln_std[:, k]))
                return tt(dst, ln_c[:, k], ln_rstd[:, k].unsqueeze(2).to_broadcast([P, NHALF * B, C]), ALU.mult)

            layernorm(0, x1[:, :, :], t1[:, :, :]).then_inc(t1_ready, 1)
            dve.wait_ge(o_done, 1)
            link(nc.vector.reciprocal(o_rec[:, :, :], o_ps[:, :, :, C]))
            link(tt(o_n[:, :, :, :], o_ps[:, :, :, 0:C], o_rec[:, :, :].unsqueeze(3).to_broadcast([P, NHALF, B, C]),
                    ALU.mult))
            tt(x2[:, :, :], x1[:, :, :], o_n[:, :, :, :].rearrange("p h b c -> p (h b) c"), ALU.add).then_inc(x2_ready, 1)
            dve.wait_ge(x2_ready, 1)
            layernorm(1, x2[:, :, :], t2[:, :, :]).then_inc(t2_ready, 1)
            dve.wait_ge(g_done, 1)
            link(ts(g_log[:, :], g_ps, weight("gate_b"), None, ALU.add))
            nc.vector.tensor_reduce(g_max[:, :], g_log[:, :], AX.X, ALU.max, negate=True).then_inc(g_max_ready, 1)
            dve.wait_ge(g_exp_ready, 1)
            link(nc.vector.reciprocal(g_rec[:, :], g_sum[:, :]))
            link(ts(g_prob[:, :], g_exp[:, :], g_rec[:, 0:1], None, ALU.mult))
            link(nc.vector.max(top[:, :], g_prob[:, :]))
            link(nc.vector.match_replace(rest[:, :], top[:, :], g_prob[:, :], 0.0))
            tt(picked[:, :], g_prob[:, :], rest[:, :], ALU.subtract).then_inc(picked_ready, 1)
            dve.wait_ge(picked_turned, 1)
            nc.vector.tensor_copy(picked_t[:, :, :], pickt_ps).then_inc(picked_copied, 1)
            dve.wait_ge(pooled_done, 1)
            nc.vector.tensor_copy(pooled[0:C, :], pool_ps).then_inc(pooled_ready, 1)
            dve.wait_ge(out2t_done, 1)
            nc.vector.tensor_copy(out2_t[:, :], b67[0:C, 512:512 + P]).then_inc(out2t_copied, 1)
            dve.wait_ge(out2_done, 1)
            link(tt(out2[:, :], out2_ps, weight("bias2"), ALU.add))
            tt(out2_blk[:, :, :], out2[:, :].unsqueeze(1).to_broadcast([P, B, C]),
               same_b.unsqueeze(2).to_broadcast([P, B, C]), ALU.mult).then_inc(out2_ready, 1)
            dve.wait_ge(y_done, 1)
            nc.vector.tensor_copy(y_sb[:, 0, :], y_ps[:, 0]).then_inc(y_ready, 1)


def kernel(x, L0_conv_w_dw, L0_conv_ln_w, L0_conv_w_off, L0_conv_wq, L0_conv_wk, L0_conv_wv, L0_conv_wo, L0_conv_rpe,
           L1_ffn_gate_w, L1_ffn_gate_b, L1_ffn_weight1, L1_ffn_weight2):
    import concourse.bacc as bacc
    from concourse.bass_utils import run_bass_kernel_spmd

    x_rows = np.ascontiguousarray(np.asarray(x).reshape(B, G, GC, M).transpose(1, 0, 2, 3).reshape(G, P, M))
    w = np.zeros((P, NWEIGHT), np.float32)

    def put(name, a):
        lo, hi = WEIGHT_COLS[name]
        a = np.asarray(a).reshape(len(a), -1)
        w[:, lo:hi] = np.tile(a, (P // len(a), 1))

    put("dw", np.asarray(L0_conv_w_dw).reshape(GC, KS * KS))
    put("ln_w", np.asarray(L0_conv_ln_w).reshape(GC, 1))
    put("w_off", np.asarray(L0_conv_w_off).T)
    proj = np.stack([np.asarray(a) for a in (L0_conv_wq, L0_conv_wk, L0_conv_wv, L0_conv_wo)])
    put("proj", proj.reshape(4, C, G, GC).transpose(3, 0, 2, 1))
    table = np.zeros((RPAD, G * HG, RPAD), np.float32)
    table[:RPE, :, :RPE] = np.asarray(L0_conv_rpe).transpose(1, 0, 2)
    put("rpe", table)
    put("gate_w", np.asarray(L1_ffn_gate_w).T)
    put("gate_b", np.asarray(L1_ffn_gate_b).reshape(NE, 1))
    put("bias2", np.asarray(L1_ffn_weight2)[:, HID, :])
    arrays = {
        "x_rows": x_rows,
        "shape_consts": shape_constants(),
        "weights": w,
        "weight1": np.ascontiguousarray(L1_ffn_weight1),
        "weight2": np.ascontiguousarray(L1_ffn_weight2),
    }
    nc = bacc.Bacc("TRN2", target_bir_lowering=False, num_devices=1)
    args = [nc.dram_tensor(name, a.shape, mybir.dt.from_np(a.dtype), kind="ExternalInput").ap()
            for name, a in arrays.items()]
    y = nc.dram_tensor("y", (NT, P, M), F32, kind="ExternalOutput").ap()
    build(nc, *args, y)
    r = run_bass_kernel_spmd(nc, [arrays], core_ids=[0])
    return np.asarray(r.results[0]["y"]).reshape(B, C, IMG, IMG)
```

```python
from contextlib import ExitStack

import numpy as np

import concourse.bass as bass
from concourse import mybir

F32 = mybir.dt.float32
BF16 = mybir.dt.bfloat16
U32 = mybir.dt.uint32
ALU = mybir.AluOpType
ACT = mybir.ActivationFunctionType
AX = mybir.AxisListType

P = 128
B, C = 8, 32
IMG = 16
M = IMG * IMG
NHALF = M // P
G = 2
GC = C // G
HG = 2
DH = C // (G * HG)
KS, STRIDE, PAD = 5, 4, 2
PADIMG = IMG + 2 * PAD
NK = IMG // STRIDE
N = NK * NK
RPE = 2 * IMG - 1
RPAD = RPE + 1
WIN = 24
NE, HID = 16, 128
E4 = P // C
EQ = NE // E4
TOPK = 8
NT = 2
B4 = B // NT
EPS = 1e-5
BUSY = [30, 10, 12, 12, 25, 20, 10, 10, 10, 30, 30, 10, 52, 20, 5, 5, 15, 10, 5]
QK_SCALE = float(DH) ** -0.5
OFFSET = 1.0 / NK * 0.5 * (IMG - 1)
SCORE_BOUND = float(C)



def columns(*widths):
    places, at = {}, 0
    for name, width in widths:
        places[name] = (at, at + width)
        at += width
    return places, at


CONST_COLS, NCONST = columns(
    ("same_b", B), ("eps", 1), ("one", 1), ("bound", 1), ("head", HG), ("ref_x", 1),
    ("ident", P), ("center", P), ("avg", P),
    ("same_b4", NT * B), ("frac_x", IMG), ("steps", 16), ("signs", 5 * 16), ("sample", 3 * N), ("rel_y", 4 * N))
CONST_CUTS = (0, CONST_COLS["ident"][0], CONST_COLS["same_b4"][0], NCONST)

WEIGHT_COLS, NWEIGHT = columns(
    ("wq", G * C), ("dw", KS * KS), ("ln_w", 1), ("w_off", 3), ("wkvo", 3 * G * C), ("rpe", G * HG * RPAD),
    ("gate_w", NE), ("gate_b", 1), ("bias1", NE), ("bias2", C))
WEIGHT_CUT = WEIGHT_COLS["wkvo"][0]


def shape_constants():
    c = np.zeros((P, NCONST), np.float32)

    def put(name, a):
        lo, hi = CONST_COLS[name]
        c[:, lo:hi] = np.broadcast_to(np.asarray(a, np.float64).reshape(len(a), -1), (P, hi - lo))

    p = np.arange(P)
    avg = (p[:, None] // GC == p[None, :] // GC) / GC
    put("avg", avg)
    put("center", np.eye(P) - avg)
    put("ident", np.eye(P))
    put("same_b", p[:, None] // GC == np.arange(B)[None, :])
    put("head", (p[:, None] % GC) // DH == np.arange(HG)[None, :])
    put("eps", np.full((P, 1), EPS))
    put("one", np.ones((P, 1)))
    put("bound", np.full((P, 1), -SCORE_BOUND))
    ref = (np.arange(NK) + 0.5) / NK * 2 - 1
    ref_y, ref_x = np.repeat(ref, NK), np.tile(ref, NK)
    half = 0.5 * (IMG - 1)
    query = (np.arange(IMG) + 0.5) / IMG * 2 - 1
    put("ref_x", (half * (query[0] - ref_x) + IMG - 1)[p % N][:, None])
    put("frac_x", (np.arange(IMG) / IMG)[None, :] * np.ones((P, 1)))
    k = np.arange(16)
    put("steps", np.where(k == 0, 1e9, k)[None, :] * np.ones((P, 1)))
    signs = np.zeros((5, 16))
    for row, bit in enumerate((8, 4, 2, 1)):
        for j in range(bit, 16, bit):
            signs[row, j] = 1 if (j // bit) % 2 else -1
    signs[4, 1:] = 1
    put("signs", signs.reshape(1, -1) * np.ones((P, 1)))
    s = np.zeros((P, 3, N))
    for h in range(NHALF):
        s[:, h] = (p // IMG + h * (P // IMG))[:, None] - half * (ref_y + 1)[None, :]
    s[:, 2] = (p % IMG)[:, None] - half * (ref_x + 1)[None, :]
    put("sample", s)
    r = np.zeros((P, 4, N))
    for yq in range(4):
        y = 4 * yq + p // 32
        r[:, yq] = (half * query[y] + IMG - 1 - p % 32)[:, None] - half * ref_y[None, :]
    put("rel_y", r)
    put("same_b4", (p[:, None] // C + B4 * (np.arange(NT * B) // B)[None, :]) == (np.arange(NT * B) % B)[None, :])
    return c


def build(nc, x_in, consts_in, weights_in, w1_in, w2_in, out):
    with ExitStack() as ctx:
        def sb(name, shape, dt=F32):
            return ctx.enter_context(nc.sbuf_tensor(name, shape, dt))

        def bank(name, n=1):
            return ctx.enter_context(nc.psum_tensor(name, [P, n * 512], F32))

        def sem(name):
            return ctx.enter_context(nc.semaphore(name))

        ps = ctx.enter_context(nc.psum_tensor("ps", [P, 8 * 512], F32))

        def bank(n, cols=512):
            return ps[:, 512 * n:512 * n + cols]

        x_sb = sb("x_sb", [P, G, M])
        cst = sb("cst", [P, NCONST])
        wts = sb("wts", [P, NWEIGHT])
        w1_sb = sb("w1_sb", [P, EQ, HID])
        w2_sb = sb("w2_sb", [HID, NE, C])

        def const(name):
            lo, hi = CONST_COLS[name]
            return cst[:, lo:hi]

        def weight(name):
            lo, hi = WEIGHT_COLS[name]
            return wts[:, lo:hi]

        ident, same_b = const("ident"), const("same_b")
        wq = weight("wq").rearrange("p (g o) -> p g o", g=G)
        wkvo = weight("wkvo").rearrange("p (w g o) -> p w g o", w=3, g=G)

        stats = sb("stats", [P, G, 6])
        meanvar = sb("meanvar", [P, G, 2])
        gn_std = sb("gn_std", [P, G])
        gn_rstd = sb("gn_rstd", [P, G])
        xn = sb("xn", [P, G, M])
        xn_tok = sb("xn_tok", [P, NHALF, G, P])
        x_tok = sb("x_tok", [P, NHALF, B, G, GC])
        wk_s = sb("wk_s", [P, G, C])
        wblk = sb("wblk", [P, 3, G, G, B, GC])
        woblk = sb("woblk", [P, G, B, C])
        gate_blk = sb("gate_blk", [P, NT, B, NE])
        rpe_blk = sb("rpe_blk", [P, G, 4, HG * RPAD])
        q_sb = sb("q_sb", [P, G, M])
        qpad = sb("qpad", [P, G, PADIMG, PADIMG])
        taps = sb("taps", [P, G, NK, NK, KS * KS])
        off = sb("off", [P, G * N])
        off_sq = sb("off_sq", [P, G * N])
        off_std = sb("off_std", [P, G * N])
        off_rstd = sb("off_rstd", [P, G * N])
        off_w = sb("off_w", [P, G * N])
        off_n = sb("off_n", [P, G * N])
        off_act = sb("off_act", [P, G * N])
        off_blk = sb("off_blk", [P, G, B, N])
        warm = sb("warm", [P, 8])
        zeros = sb("zeros", [P, P], BF16)
        th = sb("th", [P, 2, G * B * N])
        half_tanh = sb("half_tanh", [P, G * B * N])
        gate = sb("gate", [P, G * B * N])
        gate_m = sb("gate_m", [P, G, B, N])
        z_rel = sb("z_rel", [P, 4, G * B * N])
        a_rel = sb("a_rel", [P, 4, G * B * N])
        hat_rel = sb("hat_rel", [P, 4, G * B * N])
        z_smp = sb("z_smp", [P, 3, G * B * N])
        a_smp = sb("a_smp", [P, 3, G * B * N])
        hat_smp = sb("hat_smp", [P, 3, G * B * N])
        w_smp = sb("w_smp", [P, NHALF, G * B * N])
        xs = sb("xs", [P, G, B * N])
        kv = sb("kv", [P, HG, 2, G, B * N])
        vo = sb("vo", [P, G * HG, B * C])
        txh = sb("txh", [P, G])
        tx = sb("tx", [P, G])
        over = sb("over", [P, G, 16])
        signed = sb("signed", [P, G, 5, 16])
        bits = sb("bits", [P, G, 5])
        masks = sb("masks", [P, G, 5], U32)
        frac = sb("frac", [P, G])
        dist = sb("dist", [P, G, IMG])
        tap_next = sb("tap_next", [P, G, IMG])
        tap_prev = sb("tap_prev", [P, G, IMG])
        tap_nabs = sb("tap_nabs", [P, G, IMG])
        tap_here = sb("tap_here", [P, G, IMG])
        win = sb("win", [P, G, IMG * HG, WIN])
        prod = sb("prod", [P, G, 3, IMG * HG, IMG])
        bias = sb("bias", [P, G, HG, IMG, IMG])
        d_max = sb("d_max", [P, NHALF, 32])
        d_sub = sb("d_sub", [P, NHALF, 32, N])
        d_exp = sb("d_exp", [P, NHALF, 32, N])
        d_sum = sb("d_sum", [P, NHALF, 32])
        d_rec = sb("d_rec", [P, NHALF, 32])
        d_prob = sb("d_prob", [P, NHALF, 32, N])
        prob_t = sb("prob_t", [P, NHALF, G * HG, P])
        x1 = sb("x1", [P, NHALF, B, C])
        x2 = sb("x2", [P, NHALF, B, C])
        ln_sum = sb("ln_sum", [P, 2, NHALF, B])
        ln_c = sb("ln_c", [P, 2, NHALF, B, C])
        ln_sq = sb("ln_sq", [P, 2, NHALF, B, C])
        ln_ss = sb("ln_ss", [P, 2, NHALF, B])
        ln_std = sb("ln_std", [P, 2, NHALF, B])
        ln_rstd = sb("ln_rstd", [P, 2, NHALF, B])
        t1 = sb("t1", [P, NHALF, B, C])
        t1_t = sb("t1_t", [P, NT, M])
        t1_blk = sb("t1_blk", [P, NT, B4, M])
        e_tok = sb("e_tok", [P, B // 2, NHALF, 2, M])
        e_sum = sb("e_sum", [P, B // 2, NHALF, 2])
        e_rec = sb("e_rec", [P, B // 2, NHALF, 2])
        ot = sb("ot", [P, NT, M])
        o_n = sb("o_n", [P, NHALF, B, C])
        t2 = sb("t2", [P, NHALF, B, C])
        t2_t = sb("t2_t", [P, NT, M])
        g_log = sb("g_log", [P, M])
        g_max = sb("g_max", [P, 1])
        g_exp = sb("g_exp", [P, M])
        g_sum = sb("g_sum", [P, 1])
        g_rec = sb("g_rec", [P, 1])
        g_prob = sb("g_prob", [P, M])
        top = sb("top", [P, TOPK])
        rest = sb("rest", [P, M])
        picked = sb("picked", [P, M])
        picked_t = sb("picked_t", [P, NHALF, P])
        pooled = sb("pooled", [P, EQ, E4, B])
        hidden_in = sb("hidden_in", [P, NE, B])
        hidden = sb("hidden", [P, NE, B])
        out2_t = sb("out2_t", [C, P])
        out2 = sb("out2", [P, C])
        out2_blk = sb("out2_blk", [P, B, C])
        y_sb = sb("y_sb", [P, NT, M])

        xnt_ps = bank(0).rearrange("p (h g c) -> p h g c", h=NHALF, g=G)
        xt_ps = bank(1).rearrange("p (h g b c) -> p h g b c", h=NHALF, g=G, b=B)
        off_ps = [bank(n, G * B * N) for n in (0, 1, 4)]
        row_ps = [ps[:, 1024 * g:1024 * g + 1024].rearrange("p (r c) -> p r c", c=RPAD) for g in range(G)]
        pt_ps = ps[:, 0:1024].rearrange("p (h k m) -> p h k m", h=NHALF, m=P)
        t1t_ps = [bank(t, M) for t in range(NT)]
        ot_ps = [bank(t, M) for t in range(NT)]
        y_ps = [bank(t, M) for t in range(NT)]
        q_ps = [bank(2 + g, M) for g in range(G)]
        att_ps = [bank(2 + h, B * C) for h in range(NHALF)]
        t2t_ps = bank(2).rearrange("p (t m) -> p t m", t=NT)
        g_ps = bank(3, M)
        xs_ps = bank(4, G * P).rearrange("p (g n) -> p g n", g=G)
        kv_ps = bank(5).rearrange("p (w g n) -> p w g n", w=2, g=G)
        vo_ps = ps[:, 2048:3072].rearrange("p (k j) -> p k j", k=G * HG)
        masks_ps = bank(0, G * 5).bitcast(U32).rearrange("p (g k) -> p g k", g=G)
        o_ps = [bank(4 + h, B * C).rearrange("p (b c) -> p b c", b=B) for h in range(NHALF)]
        pickt_ps = bank(4, 256).rearrange("p (h k) -> p h k", h=NHALF)
        out2_ps = bank(4, C)
        pool_ps = bank(5, P)[0:C]
        cen_ps = bank(6, G * N)
        var_ps = bank(7, G * N)
        tx_ps = ps[:, 7 * 512 + 64:7 * 512 + 64 + G]
        lg_ps = ps[:, 3072:4096].rearrange("p (h k j) -> p h k j", h=NHALF, k=G * HG)
        hid_ps = bank(6, P).rearrange("p (q e b) -> p q e b", q=EQ, e=E4)
        out2t_ps = bank(7, P)[0:C]
        s_ps = [ps[:, 512 * n:512 * n + 1024] for n in (2, 4, 6, 2)]

        x_loaded = [sem(f"x_loaded{g}") for g in range(G)]
        const_loaded = [sem(f"const_loaded{n}") for n in range(3)]
        weights_loaded = [sem(f"weights_loaded{n}") for n in range(2)]
        w1_loaded, w2_loaded = sem("w1_loaded"), sem("w2_loaded")
        stored = sem("stored")
        dve_step, pool_step, act_step = sem("dve_step"), sem("pool_step"), sem("act_step")
        gn_var_ready, gn_std_ready, xn_ready = sem("gn_var_ready"), sem("gn_std_ready"), sem("xn_ready")
        wq_ready, wkvo_ready, gate_blk_ready = sem("wq_ready"), sem("wkvo_ready"), sem("gate_blk_ready")
        rpe_blk_ready, qpad_zeroed = sem("rpe_blk_ready"), sem("qpad_zeroed")
        t1_blk_zeroed, pooled_zeroed, zeros_set = sem("t1_blk_zeroed"), sem("pooled_zeroed"), sem("zeros_set")
        q_done, qpad_copied, q_copied = sem("q_done"), sem("qpad_copied"), sem("q_copied")
        x_turned, xn_turned = sem("x_turned"), sem("xn_turned")
        xn_tok_copied, x_tok_copied = sem("xn_tok_copied"), sem("x_tok_copied")
        off_ready = sem("off_ready")
        centered, squared, var_done = sem("centered"), sem("squared"), sem("var_done")
        off_std_ready, off_n_ready, off_act_ready = sem("off_std_ready"), sem("off_n_ready"), sem("off_act_ready")
        off_blk_ready, off_done = sem("off_blk_ready"), sem("off_done")
        tanh_ready, txh_ready, half_tanh_ready = sem("tanh_ready"), sem("txh_ready"), sem("half_tanh_ready")
        z_smp_ready, hat_smp_ready = sem("z_smp_ready"), sem("hat_smp_ready")
        w_smp_ready, gate_m_ready = sem("w_smp_ready"), sem("gate_m_ready")
        z_rel_ready, hat_rel_ready = sem("z_rel_ready"), sem("hat_rel_ready")
        sampled, xs_ready, kv_done, kv_ready = sem("sampled"), sem("xs_ready"), sem("kv_done"), sem("kv_ready")
        vo_done, vo_copied = sem("vo_done"), sem("vo_copied")
        rows_done, win_copied, rows_used = sem("rows_done"), sem("win_copied"), sem("rows_used")
        shifts_done, right_ready, left_edge_zeroed = sem("shifts_done"), sem("right_ready"), sem("left_edge_zeroed")
        bias0_ready, bias1_ready = sem("bias0_ready"), sem("bias1_ready")
        logits_done, d_sub_ready = sem("logits_done"), sem("d_sub_ready")
        d_exp_ready, d_prob_ready = sem("d_exp_ready"), sem("d_prob_ready")
        prob_turned, prob_copied, att_done = sem("prob_turned"), sem("prob_copied"), sem("att_done")
        ln_c_ready, ln_sq_ready, ln_ss_ready, ln_std_ready = (
            sem("ln_c_ready"), sem("ln_sq_ready"), sem("ln_ss_ready"), sem("ln_std_ready"))
        t1_ready, t1_turned = sem("t1_ready"), sem("t1_turned")
        t1_copied = [sem(f"t1_copied{t}") for t in range(NT)]
        scores_done, exp_ready = sem("scores_done"), sem("exp_ready")
        ot_done, ot_copied, o_turned, x2_ready = sem("ot_done"), sem("ot_copied"), sem("o_turned"), sem("x2_ready")
        t2_ready, t2_turned, t2_copied, g_done = sem("t2_ready"), sem("t2_turned"), sem("t2_copied"), sem("g_done")
        g_max_ready, g_exp_ready = sem("g_max_ready"), sem("g_exp_ready")
        picked_ready, picked_turned, picked_copied = sem("picked_ready"), sem("picked_turned"), sem("picked_copied")
        pooled_done, pooled_ready, hidden_done = sem("pooled_done"), sem("pooled_ready"), sem("hidden_done")
        hidden_in_ready, hidden_ready = sem("hidden_in_ready"), sem("hidden_ready")
        out2t_done, out2t_copied, out2_done, out2_ready = (
            sem("out2t_done"), sem("out2t_copied"), sem("out2_done"), sem("out2_ready"))
        y_done, y_ready = sem("y_done"), sem("y_ready")

        def conv_view(g, i):
            rows = qpad[:, g, STRIDE * i:STRIDE * i + KS, :]
            return bass.AP(tensor=rows.tensor, offset=rows.offset,
                           ap=[list(rows.ap[0]), [STRIDE, NK], [PADIMG, KS], [1, KS]])

        block = ctx.enter_context(nc.Block())

        def tap_columns(w):
            return w.unsqueeze(1).to_broadcast([P, IMG * HG, w.shape[1]])

        @block.sync
        def _(sp):
            def load_const(n):
                cols = slice(CONST_CUTS[n], CONST_CUTS[n + 1])
                sp.dma_start(cst[:, cols], consts_in[:, cols]).then_inc(const_loaded[n], 16)

            sp.dma_start(x_sb[:, 0, :], x_in[0]).then_inc(x_loaded[0], 16)
            load_const(0)
            load_const(1)
            sp.dma_start(wts[:, WEIGHT_CUT:], weights_in[:, WEIGHT_CUT:]).then_inc(weights_loaded[1], 16)
            load_const(2)
            sp.dma_start(w1_sb[:, :, :], w1_in).then_inc(w1_loaded, 16)
            sp.wait_ge(y_ready, 1)
            sp.dma_start(out[0], y_sb[:, 0, :]).then_inc(stored, 16)
            sp.wait_ge(stored, 32)

        @block.gpsimd
        def _(pool):
            steps = [0]

            def link(ins):
                steps[0] += 1
                ins.then_inc(pool_step, 1)
                pool.wait_ge(pool_step, steps[0])

            nc.gpsimd.memset(qpad[:, :, :, :], 0.0).then_inc(qpad_zeroed, 1)
            nc.gpsimd.memset(prod[:, :, 1, :, 0:1], 0.0).then_inc(left_edge_zeroed, 1)
            nc.gpsimd.memset(pooled[:, :, :, :], 0.0).then_inc(pooled_zeroed, 1)

            def pool_mult(dst, a, b):
                return nc.gpsimd.tensor_tensor(dst, a, b, ALU.mult)

            def blocks(dst, src, n_groups, width):
                return nc.gpsimd.tensor_tensor(
                    dst, src.unsqueeze(2).to_broadcast([P, n_groups, B, width]),
                    same_b.unsqueeze(1).unsqueeze(3).to_broadcast([P, n_groups, B, width]), ALU.mult)

            pool.wait_ge(weights_loaded[0], 16)
            pool.wait_ge(const_loaded[0], 16)
            blocks(wblk[:, 0, 1], wq[:, 1].rearrange("p (g o) -> p g o", g=G), G, GC).then_inc(wq_ready, 1)
            pool.wait_ge(weights_loaded[1], 16)
            pool.wait_ge(const_loaded[2], 16)
            same_b4 = const("same_b4").rearrange("p (t b) -> p t b", t=NT)
            rpe = weight("rpe").rearrange("p (g k) -> p g k", g=G)
            nc.gpsimd.tensor_tensor(
                rpe_blk[:, :, :, :], rpe.unsqueeze(2).to_broadcast([P, G, 4, HG * RPAD]),
                same_b4[:, 0, 0:4].unsqueeze(1).unsqueeze(3).to_broadcast([P, G, 4, HG * RPAD]),
                ALU.mult).then_inc(rpe_blk_ready, 1)
            link(nc.gpsimd.tensor_scalar(wk_s[:, :, :], wkvo[:, 0], QK_SCALE, None, ALU.mult))
            for g in range(G):
                blocks(wblk[:, 1, g], wk_s[:, g].rearrange("p (g o) -> p g o", g=G), G, GC).then_inc(wkvo_ready, 1)
                blocks(wblk[:, 2, g], wkvo[:, 1, g].rearrange("p (g o) -> p g o", g=G), G, GC).then_inc(wkvo_ready, 1)
            pool.wait_ge(half_tanh_ready, 1)
            link(nc.gpsimd.tensor_scalar(gate[:, :], half_tanh[:, :], 0.5, 0.5, ALU.mult, ALU.add))
            for g in range(G):
                nc.gpsimd.tensor_tensor(
                    gate_m[:, g], gate[:, :].rearrange("p (g b n) -> p g b n", g=G, b=B)[:, g],
                    same_b.unsqueeze(2).to_broadcast([P, B, N]), ALU.mult).then_inc(gate_m_ready, 1)
            pool.wait_ge(hat_smp_ready, 1)
            for h in range(NHALF):
                nc.gpsimd.tensor_tensor(w_smp[:, h], hat_smp[:, h], hat_smp[:, 2], ALU.mult).then_inc(w_smp_ready, 1)
            for g in range(G):
                blocks(woblk[:, g].unsqueeze(1), wkvo[:, 2, g].unsqueeze(1), 1, C).then_inc(wkvo_ready, 1)
            pool.wait_ge(shifts_done, 1)
            here, left, right = (prod[:, 0, n] for n in range(3))
            pool_mult(here, win[:, 0, :, 0:IMG], tap_columns(tap_here[:, 0]))
            link(pool_mult(left[:, :, 1:IMG], win[:, 0, :, 0:IMG - 1], tap_columns(tap_prev[:, 0, 1:IMG])))
            pool.wait_ge(right_ready, 1)
            link(nc.gpsimd.tensor_tensor(here, here, right, ALU.add))
            out_0 = bias[:, 0].rearrange("p h y x -> p y h x")
            rows = "p (y h) x -> p y h x"
            nc.gpsimd.tensor_tensor(out_0, here.rearrange(rows, h=HG), left.rearrange(rows, h=HG),
                                    ALU.add).then_inc(bias0_ready, 1)
            nc.gpsimd.memset(t1_blk[:, :, :, :], 0.0).then_inc(t1_blk_zeroed, 1)
            nc.gpsimd.tensor_tensor(
                gate_blk[:, :, :, :], weight("gate_w").unsqueeze(1).unsqueeze(1).to_broadcast([P, NT, B, NE]),
                same_b4.unsqueeze(3).to_broadcast([P, NT, B, NE]), ALU.mult).then_inc(gate_blk_ready, 1)

        @block.scalar
        def _(act):
            act.dma_start(x_sb[:, 1, :], x_in[1]).then_inc(x_loaded[1], 16)
            act.dma_start(wts[:, 0:WEIGHT_CUT], weights_in[:, 0:WEIGHT_CUT]).then_inc(weights_loaded[0], 16)
            act.dma_start(w2_sb[:, :, :], w2_in[:, 0:HID, :].rearrange("e h o -> h e o")).then_inc(w2_loaded, 16)
            warmed = [0]

            def load_table(func):
                n = warmed[0]
                warmed[0] += 1
                nc.scalar.activation(warm[:, n:n + 1], const("one"), func)

            act.wait_ge(const_loaded[0], 16)
            load_table(ACT.Sqrt)
            act.wait_ge(gn_var_ready, 1)
            nc.scalar.activation(gn_std[:, :], meanvar[:, :, 1], ACT.Sqrt, bias=const("eps")).then_inc(gn_std_ready, 1)
            act.wait_ge(x_turned, 1)
            for h in range(NHALF):
                nc.scalar.activation(x_tok[:, h].rearrange("p b g c -> p g b c"), xt_ps[:, h],
                                     ACT.Copy).then_inc(x_tok_copied, 1)
            act.wait_ge(qpad_zeroed, 1)
            for g in range(G):
                act.wait_ge(q_done, g + 1)
                nc.scalar.activation(qpad[:, g, PAD:PAD + IMG, PAD:PAD + IMG],
                                     q_ps[g].rearrange("p (y x) -> p y x", y=IMG), ACT.Copy).then_inc(qpad_copied, 1)
            for g in range(G):
                nc.scalar.activation(q_sb[:, g], q_ps[g], ACT.Copy).then_inc(q_copied, 1)
            act.wait_ge(xn_turned, 1)
            nc.scalar.activation(xn_tok[:, :, :, :], xnt_ps, ACT.Copy).then_inc(xn_tok_copied, 1)
            act.wait_ge(centered, 1)
            nc.scalar.activation(off_sq[:, :], cen_ps, ACT.Square).then_inc(squared, 1)
            act.wait_ge(var_done, 1)
            nc.scalar.activation(off_std[:, :], var_ps, ACT.Sqrt, bias=const("eps")).then_inc(off_std_ready, 1)
            load_table(ACT.Gelu)
            act.wait_ge(off_n_ready, 1)
            nc.scalar.activation(off_act[:, :], off_n[:, :], ACT.Gelu).then_inc(off_act_ready, 1)
            for j in range(2):
                act.wait_ge(off_done, j + 1)
                nc.scalar.activation(th[:, j], off_ps[j], ACT.Tanh).then_inc(tanh_ready, 1)
            act.wait_ge(off_done, 3)
            nc.scalar.activation(txh[:, :], tx_ps, ACT.Tanh).then_inc(txh_ready, 1)
            for k in range(2):
                act.wait_ge(z_rel_ready, 2 * k + 2)
                nc.scalar.activation(a_rel[:, 2 * k:2 * k + 2], z_rel[:, 2 * k:2 * k + 2], ACT.Abs).then_inc(act_step, 1)
            for k in range(2):
                act.wait_ge(act_step, k + 1)
                nc.scalar.activation(hat_rel[:, 2 * k:2 * k + 2], a_rel[:, 2 * k:2 * k + 2], ACT.Relu,
                                     bias=const("one"), scale=-1.0).then_inc(hat_rel_ready, 1)
            act.wait_ge(off_done, 4)
            nc.scalar.activation(half_tanh[:, :], off_ps[2], ACT.Tanh, scale=0.5).then_inc(half_tanh_ready, 1)
            act.wait_ge(z_smp_ready, 3)
            nc.scalar.activation(a_smp[:, :, :], z_smp[:, :, :], ACT.Abs).then_inc(act_step, 1)
            act.wait_ge(act_step, 3)
            nc.scalar.activation(hat_smp[:, :, :], a_smp[:, :, :], ACT.Relu, bias=const("one"),
                                 scale=-1.0).then_inc(hat_smp_ready, 1)
            for g in range(G):
                act.wait_ge(rows_done, g + 1)
                nc.scalar.activation(win[:, g], row_ps[g][:, :, 0:WIN], ACT.Copy).then_inc(win_copied, 1)
            load_table(ACT.Exp)
            act.wait_ge(kv_done, 1)
            for hh in range(HG):
                nc.scalar.activation(kv[:, hh].rearrange("p w g n -> p (w g n)"), bank(5), ACT.Copy,
                                     scale=const("head")[:, hh:hh + 1]).then_inc(kv_ready, 1)
            act.wait_ge(vo_done, 1)
            nc.scalar.activation(vo[:, :, :], vo_ps, ACT.Copy).then_inc(vo_copied, 1)
            for h in range(NHALF):
                act.wait_ge(d_sub_ready, h + 1)
                nc.scalar.activation(d_exp[:, h], d_sub[:, h], ACT.Exp).then_inc(d_exp_ready, 1)
            load_table(ACT.Sqrt)
            for h in range(NHALF):
                act.wait_ge(prob_turned, h + 1)
                nc.scalar.activation(prob_t[:, h], pt_ps[:, h], ACT.Copy).then_inc(prob_copied, 1)

            def layernorm(k):
                for h in range(NHALF):
                    act.wait_ge(ln_c_ready, NHALF * k + h + 1)
                    nc.scalar.activation(ln_sq[:, k, h], ln_c[:, k, h], ACT.Square).then_inc(ln_sq_ready, 1)
                for h in range(NHALF):
                    act.wait_ge(ln_ss_ready, NHALF * k + h + 1)
                    nc.scalar.activation(ln_std[:, k, h], ln_ss[:, k, h], ACT.Sqrt, bias=const("eps"),
                                         scale=1.0 / C).then_inc(ln_std_ready, 1)

            layernorm(0)
            load_table(ACT.Exp)
            act.wait_ge(t1_turned, 1)
            act.wait_ge(t1_blk_zeroed, 1)
            nc.scalar.activation(t1_t[:, 0], t1t_ps[0], ACT.Copy).then_inc(t1_copied[0], 1)
            for b in range(B4):
                rows = slice(C * b, C * b + C)
                nc.scalar.activation(t1_blk[rows, 0, b], t1t_ps[0][rows], ACT.Copy).then_inc(t1_copied[0], 1)
            for n in range(B // 2):
                act.wait_ge(scores_done, n + 1)
                parts = 1 if n < B // 2 - 1 else 2
                for k in range(parts):
                    cols = slice(k * 1024 // parts, (k + 1) * 1024 // parts)
                    nc.scalar.activation(e_tok[:, n].rearrange("p h b q -> p (h b q)")[:, cols], s_ps[n][:, cols],
                                         ACT.Exp, bias=const("bound")).then_inc(exp_ready, 1)
                if n == 2:
                    act.wait_ge(ot_done, 1)
                    nc.scalar.activation(ot[:, 0], ot_ps[0], ACT.Copy).then_inc(ot_copied, 1)
            act.wait_ge(ot_done, 2)
            nc.scalar.activation(ot[:, 1], ot_ps[1], ACT.Copy).then_inc(ot_copied, 1)
            load_table(ACT.Sqrt)
            layernorm(1)
            load_table(ACT.Exp)
            act.wait_ge(t2_turned, 1)
            nc.scalar.activation(t2_t[:, :, :], t2t_ps, ACT.Copy).then_inc(t2_copied, 1)
            act.wait_ge(g_max_ready, 1)
            nc.scalar.activation(g_exp[:, :], g_log[:, :], ACT.Exp, bias=g_max[:, 0:1],
                                 accum_out=g_sum[:, 0:1]).then_inc(g_exp_ready, 1)
            load_table(ACT.Gelu)
            act.wait_ge(hidden_in_ready, 1)
            nc.scalar.activation(hidden[:, :, :], hidden_in[:, :, :], ACT.Gelu).then_inc(hidden_ready, 1)
            act.wait_ge(y_done, 2)
            nc.scalar.activation(y_sb[:, 1, :], y_ps[1], ACT.Copy).then_inc(act_step, 1)
            act.wait_ge(act_step, 4)
            act.dma_start(out[1], y_sb[:, 1, :]).then_inc(stored, 16)

        @block.tensor
        def _(pe):
            mm = nc.tensor.matmul

            def keep_busy(n, n_bank):
                for _ in range(n):
                    mm(bank(n_bank, P), zeros[:, :], zeros[:, :], start=True, stop=True)

            pe.wait_ge(zeros_set, 1)
            keep_busy(BUSY[0], 7)
            pe.wait_ge(const_loaded[1], 16)
            for g in range(G):
                pe.wait_ge(x_loaded[g], 16)
                for h in range(NHALF):
                    last = nc.tensor.transpose(xt_ps[:, h, g].rearrange("p b c -> p (b c)"),
                                               x_sb[:, g, h * P:(h + 1) * P], ident)
            last.then_inc(x_turned, 1)
            keep_busy(BUSY[1], 7)
            pe.wait_ge(wq_ready, 2)
            pe.wait_ge(xn_ready, 2)
            for g in range(G):
                for gi in range(G):
                    last = mm(q_ps[g], wblk[:, 0, gi, g].rearrange("p b o -> p (b o)"), xn[:, gi],
                              start=(gi == 0), stop=(gi == G - 1))
                last.then_inc(q_done, 1)
            for h in range(NHALF):
                for g in range(G):
                    last = nc.tensor.transpose(xnt_ps[:, h, g], xn[:, g, h * P:(h + 1) * P], ident)
            last.then_inc(xn_turned, 1)
            keep_busy(BUSY[2], 7)
            pe.wait_ge(off_ready, G)
            mm(cen_ps, const("center"), off[:, :], start=True, stop=True).then_inc(centered, 1)
            pe.wait_ge(squared, 1)
            mm(var_ps, const("avg"), off_sq[:, :], start=True, stop=True).then_inc(var_done, 1)
            keep_busy(BUSY[3], 4)
            pe.wait_ge(off_blk_ready, 1)
            pe.wait_ge(xn_tok_copied, 1)
            pe.wait_ge(x_tok_copied, 2)
            cols = off_blk[:, :, :, :].rearrange("p g b n -> p (g b n)")

            def offset(j):
                return mm(off_ps[j], weight("w_off")[:, j:j + 1].to_broadcast([P, P]), cols, start=True, stop=True)

            offset(0).then_inc(off_done, 1)
            offset(1).then_inc(off_done, 1)
            for g in range(G):
                last = mm(tx_ps[:, g:g + 1], off_blk[:, g].rearrange("p b n -> p (b n)"),
                          weight("w_off")[:, 1:2], start=True, stop=True)
            last.then_inc(off_done, 1)
            offset(2).then_inc(off_done, 1)
            keep_busy(BUSY[4], 5)
            pe.wait_ge(rpe_blk_ready, 1)
            pe.wait_ge(q_copied, G)
            for g in range(G):
                for yq in range(4):
                    pe.wait_ge(hat_rel_ready, yq // 2 + 1)
                    last = mm(row_ps[g][:, 8 * yq:8 * yq + 8].rearrange("p r c -> p (r c)"),
                              hat_rel[:, yq, g * P:(g + 1) * P], rpe_blk[:, g].rearrange("p k c -> p (k c)"),
                              start=True, stop=True)
                last.then_inc(rows_done, 1)
            keep_busy(BUSY[5], 5)
            pe.wait_ge(half_tanh_ready, 1)
            pe.wait_ge(w_smp_ready, 2)
            for g in range(G):
                for h in range(NHALF):
                    last = mm(xs_ps[:, g], xn_tok[:, h, g], w_smp[:, h, g * P:(g + 1) * P],
                              start=(h == 0), stop=(h == NHALF - 1))
            last.then_inc(sampled, 1)
            keep_busy(BUSY[6], 6)
            pe.wait_ge(xs_ready, 1)
            pe.wait_ge(wkvo_ready, 4)
            for w in range(2):
                for g in range(G):
                    for gi in range(G):
                        last = mm(kv_ps[:, w, g], wblk[:, 1 + w, gi, g].rearrange("p b o -> p (b o)"), xs[:, gi],
                                  start=(gi == 0), stop=(gi == G - 1))
            last.then_inc(kv_done, 1)
            keep_busy(BUSY[7], 6)
            pe.wait_ge(kv_ready, HG)
            pe.wait_ge(txh_ready, 1)
            for h in range(NHALF):
                for g in range(G):
                    for hh in range(HG):
                        mm(lg_ps[:, h, g * HG + hh], q_sb[:, g, h * P:(h + 1) * P], kv[:, hh, 0, g],
                           start=(g + hh == 0), stop=False, skip_group_check=True)
            pe.wait_ge(wkvo_ready, 6)
            for g in range(G):
                for hh in range(HG):
                    last = mm(vo_ps[:, g * HG + hh], kv[:, hh, 1, g], woblk[:, g].rearrange("p b o -> p (b o)"),
                              start=True, stop=True)
            last.then_inc(vo_done, 1)
            pe.wait_ge(rows_used, 1)
            keep_busy(BUSY[8], 1)
            for g in range(G):
                pe.wait_ge((bias0_ready, bias1_ready)[g], 1)
                for h in range(NHALF):
                    for hh in range(HG):
                        last = mm(lg_ps[:, h, g * HG + hh],
                                  bias[:, g, hh, 8 * h:8 * h + 8].rearrange("p y x -> p (y x)"), ident,
                                  start=False, stop=True, skip_group_check=True)
                    if g == G - 1:
                        last.then_inc(logits_done, 1)
            pe.wait_ge(rows_used, G)
            keep_busy(BUSY[9], 2)
            for h in range(NHALF):
                pe.wait_ge(d_prob_ready, h + 1)
                for k in range(G * HG):
                    last = nc.tensor.transpose(
                        pt_ps[:, h, k], d_prob[:, h, 8 * k:8 * k + 8].rearrange("p b n -> p (b n)"), ident)
                last.then_inc(prob_turned, 1)
            pe.wait_ge(vo_copied, 1)
            for h in range(NHALF):
                pe.wait_ge(prob_copied, h + 1)
                for k in range(G * HG):
                    last = mm(att_ps[h], prob_t[:, h, k], vo[:, k], start=(k == 0), stop=(k == G * HG - 1))
                last.then_inc(att_done, 1)
            t1_rows = t1[:, :, :, :].rearrange("p h b c -> p h (b c)")
            keep_busy(BUSY[10], 6)
            pe.wait_ge(t1_ready, NHALF)
            for t in range(NT):
                for h in range(NHALF):
                    last = nc.tensor.transpose(t1t_ps[t][:, h * P:(h + 1) * P], t1_rows[:, h, P * t:P * t + P], ident)
                last.then_inc(t1_turned, 1)

            def scores(n):
                t, pair = n // 2, n % 2
                pe.wait_ge(t1_copied[t], 3 + 2 * pair)
                for h in range(NHALF):
                    last = mm(s_ps[n][:, 512 * h:512 * h + 512], t1_t[:, t, h * P:(h + 1) * P],
                              t1_blk[:, t, 2 * pair:2 * pair + 2].rearrange("p b q -> p (b q)"), start=True, stop=True)
                last.then_inc(scores_done, 1)

            def attend(n):
                pe.wait_ge(exp_ready, n + 1 if n < B // 2 - 1 else n + 2)
                for b in (2 * n, 2 * n + 1):
                    for h in range(NHALF):
                        rows = slice(C * (b % B4), C * (b % B4) + C)
                        last = mm(ot_ps[b // B4][rows], t1[:, h, b], e_tok[:, n, h, b % 2],
                                  start=(h == 0), stop=(h == NHALF - 1))
                if n % 2 == 1:
                    last.then_inc(ot_done, 1)

            def turn_back(t):
                pe.wait_ge(ot_copied, t + 1)
                for h in range(NHALF):
                    last = nc.tensor.transpose(bank(4 + h)[:, t * P:(t + 1) * P], ot[:, t, h * P:(h + 1) * P], ident)
                last.then_inc(o_turned, 1)

            keep_busy(BUSY[11], 6)
            scores(0)
            scores(1)
            scores(2)
            pe.wait_ge(t1_copied[1], 5)
            attend(0)
            scores(3)
            attend(1)
            attend(2)
            attend(3)
            turn_back(0)
            turn_back(1)
            keep_busy(BUSY[12], 6)
            t2_rows = t2[:, :, :, :].rearrange("p h b c -> p h (b c)")
            for h in range(NHALF):
                pe.wait_ge(t2_ready, h + 1)
                for t in range(NT):
                    last = nc.tensor.transpose(t2t_ps[:, t, h * P:(h + 1) * P], t2_rows[:, h, P * t:P * t + P], ident)
            last.then_inc(t2_turned, 1)
            pe.wait_ge(t2_copied, 1)
            pe.wait_ge(gate_blk_ready, 1)
            for t in range(NT):
                last = mm(g_ps, gate_blk[:, t].rearrange("p b e -> p (b e)"), t2_t[:, t],
                          start=(t == 0), stop=(t == NT - 1))
            last.then_inc(g_done, 1)
            x2_rows = x2[:, :, :, :].rearrange("p h b c -> p h (b c)")
            for t in range(NT):
                for h in range(NHALF):
                    mm(y_ps[t][:, h * P:(h + 1) * P], x2_rows[:, h, P * t:P * t + P], ident,
                       start=(h == 0), stop=False, skip_group_check=True)
            keep_busy(BUSY[13], 6)
            pe.wait_ge(picked_ready, 1)
            for h in range(NHALF):
                last = nc.tensor.transpose(pickt_ps[:, h], picked[:, h * P:(h + 1) * P], ident)
            last.then_inc(picked_turned, 1)
            keep_busy(BUSY[14], 6)
            pe.wait_ge(picked_copied, 1)
            for b in range(B):
                for h in range(NHALF):
                    last = mm(pool_ps[:, NE * b:NE * b + NE], t2[:, h, b, :], picked_t[:, h, NE * b:NE * b + NE],
                              start=(h == 0), stop=(h == NHALF - 1))
            last.then_inc(pooled_done, 1)
            pe.wait_ge(w1_loaded, 16)
            keep_busy(BUSY[15], 7)
            pe.wait_ge(pooled_ready, E4)
            for q in range(EQ):
                last = mm(hid_ps[:, q].rearrange("p e b -> p (e b)"), w1_sb[:, q, :],
                          pooled[:, q].rearrange("p e b -> p (e b)"), start=True, stop=True)
            last.then_inc(hidden_done, 1)
            keep_busy(BUSY[16], 5)
            pe.wait_ge(hidden_ready, 1)
            pe.wait_ge(w2_loaded, 16)
            for e in range(NE):
                last = mm(out2t_ps.rearrange("p (b e) -> p e b", e=NE)[:, e], w2_sb[:, e, :], hidden[:, e, :],
                          start=True, stop=True)
            last.then_inc(out2t_done, 1)
            keep_busy(BUSY[17], 5)
            pe.wait_ge(out2t_copied, 1)
            nc.tensor.transpose(out2_ps, out2_t[:, :], ident[0:C, 0:C]).then_inc(out2_done, 1)
            keep_busy(BUSY[18], 5)
            for t in range(NT):
                pe.wait_ge(out2_ready, t + 1)
                mm(y_ps[t], out2_blk[:, B4 * t:B4 * t + B4].rearrange("p b o -> p (b o)"), picked[:, :],
                   start=False, stop=True, skip_group_check=True).then_inc(y_done, 1)

        @block.vector
        def _(dve):
            steps = [0]

            def link(ins):
                steps[0] += 1
                ins.then_inc(dve_step, 1)
                dve.wait_ge(dve_step, steps[0])

            tt = nc.vector.tensor_tensor
            ts = nc.vector.tensor_scalar
            stt = nc.vector.scalar_tensor_tensor
            reduce = nc.vector.tensor_reduce

            nc.vector.memset(zeros[:, :], 0.0).then_inc(zeros_set, 1)
            for g in range(G):
                dve.wait_ge(x_loaded[g], 16)
                link(nc.vector.bn_stats(stats[:, g], x_sb[:, g]))
                last = nc.vector.bn_aggr(meanvar[:, g], stats[:, g])
            last.then_inc(gn_var_ready, 1)
            dve.wait_ge(weights_loaded[0], 16)
            dve.wait_ge(const_loaded[0], 16)
            tt(wblk[:, 0, 0],
               wq[:, 0].rearrange("p (g o) -> p g o", g=G).unsqueeze(2).to_broadcast([P, G, B, GC]),
               same_b.unsqueeze(1).unsqueeze(3).to_broadcast([P, G, B, GC]), ALU.mult).then_inc(wq_ready, 1)
            dve.wait_ge(gn_std_ready, 1)
            link(nc.vector.reciprocal(gn_rstd[:, :], gn_std[:, :]))
            for g in range(G):
                ts(xn[:, g], x_sb[:, g], meanvar[:, g, 0:1], gn_rstd[:, g:g + 1], ALU.subtract,
                   ALU.mult).then_inc(xn_ready, 1)
            dw = weight("dw").rearrange("p (a b) -> p a b", a=KS).unsqueeze(1).to_broadcast([P, NK, KS, KS])
            for g in range(G):
                dve.wait_ge(qpad_copied, g + 1)
                for i in range(NK):
                    last = tt(taps[:, g, i].rearrange("p j (a b) -> p j a b", a=KS), conv_view(g, i), dw, ALU.mult)
                link(last)
                reduce(off[:, g * N:(g + 1) * N], taps[:, g].rearrange("p i j k -> p (i j) k"), AX.X,
                       ALU.add).then_inc(off_ready, 1)
            dve.wait_ge(off_ready, G)
            ts(off_w[:, :], off[:, :], weight("ln_w"), None, ALU.mult)
            dve.wait_ge(off_std_ready, 1)
            link(nc.vector.reciprocal(off_rstd[:, :], off_std[:, :]))
            tt(off_n[:, :], off_w[:, :], off_rstd[:, :], ALU.mult).then_inc(off_n_ready, 1)
            dve.wait_ge(off_act_ready, 1)
            tt(off_blk[:, :, :, :],
               off_act[:, :].rearrange("p (g n) -> p g n", g=G).unsqueeze(2).to_broadcast([P, G, B, N]),
               same_b.unsqueeze(1).unsqueeze(3).to_broadcast([P, G, B, N]), ALU.mult).then_inc(off_blk_ready, 1)

            def distance(z, j, coordinates):
                return stt(out=z.rearrange("p (q n) -> p q n", n=N), in0=th[:, j].rearrange("p (q n) -> p q n", n=N),
                           scalar=-OFFSET, in1=coordinates.unsqueeze(1).to_broadcast([P, G * B, N]),
                           op0=ALU.mult, op1=ALU.add)

            dve.wait_ge(const_loaded[2], 16)
            dve.wait_ge(tanh_ready, 1)
            rel = const("rel_y").rearrange("p (k n) -> p k n", k=4)
            for k in range(4):
                distance(z_rel[:, k], 0, rel[:, k]).then_inc(z_rel_ready, 1)
            dve.wait_ge(tanh_ready, 2)
            smp = const("sample").rearrange("p (k n) -> p k n", k=3)
            for k in range(3):
                distance(z_smp[:, k], 0 if k < NHALF else 1, smp[:, k]).then_inc(z_smp_ready, 1)
            dve.wait_ge(txh_ready, 1)
            link(ts(tx[:, :], txh[:, :], -OFFSET, const("ref_x"), ALU.mult, ALU.add))
            link(tt(over[:, :, :], tx[:, :].unsqueeze(2).to_broadcast([P, G, 16]),
                    const("steps").unsqueeze(1).to_broadcast([P, G, 16]), ALU.is_ge))
            link(tt(signed[:, :, :, :], over[:, :, :].unsqueeze(2).to_broadcast([P, G, 5, 16]),
                    const("signs").rearrange("p (k j) -> p k j", k=5).unsqueeze(1).to_broadcast([P, G, 5, 16]),
                    ALU.mult))
            link(reduce(bits[:, :, :], signed[:, :, :, :], AX.X, ALU.add))
            nc.vector.tensor_copy(masks[:, :, :], bits[:, :, :])
            link(tt(frac[:, :], tx[:, :], bits[:, :, 4], ALU.subtract))
            link(tt(dist[:, :, :], frac[:, :].unsqueeze(2).to_broadcast([P, G, IMG]),
                    const("frac_x").unsqueeze(1).to_broadcast([P, G, IMG]), ALU.subtract))
            ts(tap_next[:, :, :], dist[:, :, :], 0.0, None, ALU.max)
            ts(tap_prev[:, :, :], dist[:, :, :], -1.0, 0.0, ALU.mult, ALU.max)
            link(stt(out=tap_nabs[:, :, :], in0=dist[:, :, :], scalar=-1.0, in1=dist[:, :, :], op0=ALU.mult,
                     op1=ALU.min))
            link(ts(tap_here[:, :, :], tap_nabs[:, :, :], 1.0, None, ALU.add))

            def shifts(g):
                dve.wait_ge(win_copied, g + 1)

                def shifted(width, bit, source, mask):
                    return nc.vector.copy_predicated(
                        win[:, g, :, 0:width], mask[:, g, bit:bit + 1].unsqueeze(2).to_broadcast(
                            [P, IMG * HG, width]), source)

                shifted(24, 0, row_ps[g][:, :, 8:32], masks).then_inc(rows_used, 1)
                dve.wait_ge(rows_used, g + 1)
                if g == 0:
                    link(nc.vector.tensor_copy(masks_ps, masks[:, :, :]))
                link(shifted(20, 1, win[:, g, :, 4:24], masks_ps))
                link(shifted(18, 2, win[:, g, :, 2:20], masks_ps))
                shifted(17, 3, win[:, g, :, 1:18], masks_ps).then_inc(shifts_done, 1)
                dve.wait_ge(shifts_done, g + 1)

            def right(g):
                return tt(prod[:, g, 2], win[:, g, :, 1:IMG + 1], tap_columns(tap_next[:, g]), ALU.mult)

            shifts(0)
            right(0).then_inc(right_ready, 1)
            dve.wait_ge(sampled, 1)
            dve.wait_ge(gate_m_ready, G)
            tt(xs[:, :, :], xs_ps, gate_m[:, :, :, :].rearrange("p g b n -> p g (b n)"), ALU.mult).then_inc(xs_ready, 1)
            shifts(1)
            here_1, left_1, right_1 = (prod[:, 1, n] for n in range(3))
            right(1)
            link(tt(here_1, win[:, 1, :, 0:IMG], tap_columns(tap_here[:, 1]), ALU.mult))
            dve.wait_ge(left_edge_zeroed, 1)
            tt(left_1[:, :, 1:IMG], win[:, 1, :, 0:IMG - 1], tap_columns(tap_prev[:, 1, 1:IMG]), ALU.mult)
            link(tt(here_1, here_1, right_1, ALU.add))
            rows = "p (y h) x -> p y h x"
            tt(bias[:, 1].rearrange("p h y x -> p y h x"), here_1.rearrange(rows, h=HG), left_1.rearrange(rows, h=HG),
               ALU.add).then_inc(bias1_ready, 1)
            lg_rows = [lg_ps[:, h].rearrange("p k (b n) -> p (k b) n", n=N) for h in range(NHALF)]
            for h in range(NHALF):
                dve.wait_ge(logits_done, h + 1)
                link(reduce(d_max[:, h], lg_rows[h], AX.X, ALU.max))
                tt(d_sub[:, h], lg_rows[h], d_max[:, h].unsqueeze(2).to_broadcast([P, 32, N]),
                   ALU.subtract).then_inc(d_sub_ready, 1)
            for h in range(NHALF):
                dve.wait_ge(d_exp_ready, h + 1)
                link(reduce(d_sum[:, h], d_exp[:, h], AX.X, ALU.add))
                link(nc.vector.reciprocal(d_rec[:, h], d_sum[:, h]))
                tt(d_prob[:, h], d_exp[:, h], d_rec[:, h].unsqueeze(2).to_broadcast([P, 32, N]),
                   ALU.mult).then_inc(d_prob_ready, 1)

            def by_token(a):
                return a.unsqueeze(2).to_broadcast([P, B, C])

            def center(k, h, src):
                link(reduce(ln_sum[:, k, h], src[:, h], AX.X, ALU.add))
                stt(out=ln_c[:, k, h], in0=by_token(ln_sum[:, k, h]), scalar=-1.0 / C, in1=src[:, h], op0=ALU.mult,
                    op1=ALU.add).then_inc(ln_c_ready, 1)

            def normalize(k, dst, ready):
                for h in range(NHALF):
                    dve.wait_ge(ln_sq_ready, NHALF * k + h + 1)
                    reduce(ln_ss[:, k, h], ln_sq[:, k, h], AX.X, ALU.add).then_inc(ln_ss_ready, 1)
                for h in range(NHALF):
                    dve.wait_ge(ln_std_ready, NHALF * k + h + 1)
                    dve.wait_ge(ln_c_ready, NHALF * k + h + 1)
                    link(nc.vector.reciprocal(ln_rstd[:, k, h], ln_std[:, k, h]))
                    tt(dst[:, h], ln_c[:, k, h], by_token(ln_rstd[:, k, h]), ALU.mult).then_inc(ready, 1)

            dve.wait_ge(x_tok_copied, NHALF)
            for h in range(NHALF):
                dve.wait_ge(att_done, h + 1)
                link(tt(x1[:, h].rearrange("p b c -> p (b c)"), att_ps[h],
                        x_tok[:, h].rearrange("p b g c -> p (b g c)"), ALU.add))
                center(0, h, x1)
            normalize(0, t1, t1_ready)
            dve.wait_ge(t1_turned, 2)
            dve.wait_ge(t1_blk_zeroed, 1)
            nc.vector.tensor_copy(t1_t[:, 1], t1t_ps[1]).then_inc(t1_copied[1], 1)
            for b in range(B4):
                rows = slice(C * b, C * b + C)
                nc.vector.tensor_copy(t1_blk[rows, 1, b], t1t_ps[1][rows]).then_inc(t1_copied[1], 1)
            for n in range(B // 2 - 1):
                dve.wait_ge(exp_ready, n + 1)
                reduce(e_sum[:, n], e_tok[:, n], AX.X, ALU.add)
            for h in range(NHALF):
                dve.wait_ge(exp_ready, B // 2 + h)
                last = reduce(e_sum[:, B // 2 - 1, h], e_tok[:, B // 2 - 1, h], AX.X, ALU.add)
            link(last)
            link(nc.vector.reciprocal(e_rec[:, :, :, :], e_sum[:, :, :, :]))
            dve.wait_ge(o_turned, NT)
            for h in range(NHALF):
                pairs = "p (n b) c -> p n b c"
                link(tt(o_n[:, h].rearrange(pairs, b=2), o_ps[h].rearrange(pairs, b=2),
                        e_rec[:, :, h].unsqueeze(3).to_broadcast([P, B // 2, 2, C]), ALU.mult))
                tt(x2[:, h], x1[:, h], o_n[:, h], ALU.add).then_inc(x2_ready, 1)
                dve.wait_ge(x2_ready, h + 1)
                center(1, h, x2)
            normalize(1, t2, t2_ready)
            dve.wait_ge(g_done, 1)
            link(ts(g_log[:, :], g_ps, weight("gate_b"), None, ALU.add))
            reduce(g_max[:, :], g_log[:, :], AX.X, ALU.max, negate=True).then_inc(g_max_ready, 1)
            dve.wait_ge(g_exp_ready, 1)
            link(nc.vector.reciprocal(g_rec[:, :], g_sum[:, :]))
            link(ts(g_prob[:, :], g_exp[:, :], g_rec[:, 0:1], None, ALU.mult))
            link(nc.vector.max(top[:, :], g_prob[:, :]))
            link(nc.vector.match_replace(rest[:, :], top[:, :], g_prob[:, :], 0.0))
            tt(picked[:, :], g_prob[:, :], rest[:, :], ALU.subtract).then_inc(picked_ready, 1)
            dve.wait_ge(picked_turned, 1)
            nc.vector.tensor_copy(picked_t[:, :, :], pickt_ps).then_inc(picked_copied, 1)
            dve.wait_ge(pooled_zeroed, 1)
            dve.wait_ge(pooled_done, 1)
            for e in range(E4):
                nc.vector.tensor_copy(
                    pooled[C * e:C * e + C, :, e, :],
                    pool_ps.rearrange("p (b q e) -> p e q b", q=EQ, e=E4)[:, e]).then_inc(pooled_ready, 1)
            dve.wait_ge(hidden_done, 1)
            tt(hidden_in[:, :, :], hid_ps.rearrange("p q e b -> p (q e) b"),
               weight("bias1").unsqueeze(2).to_broadcast([P, NE, B]), ALU.add).then_inc(hidden_in_ready, 1)
            dve.wait_ge(out2t_done, 1)
            nc.vector.tensor_copy(out2_t[:, :], out2t_ps).then_inc(out2t_copied, 1)
            dve.wait_ge(out2_done, 1)
            link(tt(out2[:, :], out2_ps, weight("bias2"), ALU.add))
            for t in range(NT):
                batches = slice(B4 * t, B4 * t + B4)
                tt(out2_blk[:, batches], out2[:, :].unsqueeze(1).to_broadcast([P, B4, C]),
                   same_b[:, batches].unsqueeze(2).to_broadcast([P, B4, C]), ALU.mult).then_inc(out2_ready, 1)
            dve.wait_ge(y_done, 1)
            nc.vector.tensor_copy(y_sb[:, 0, :], y_ps[0]).then_inc(y_ready, 1)


def kernel(x, L0_conv_w_dw, L0_conv_ln_w, L0_conv_w_off, L0_conv_wq, L0_conv_wk, L0_conv_wv, L0_conv_wo, L0_conv_rpe,
           L1_ffn_gate_w, L1_ffn_gate_b, L1_ffn_weight1, L1_ffn_weight2):
    import concourse.bacc as bacc
    from concourse.bass_utils import run_bass_kernel_spmd

    x_rows = np.ascontiguousarray(np.asarray(x).reshape(B, G, GC, M).transpose(1, 0, 2, 3).reshape(G, P, M))
    w = np.zeros((P, NWEIGHT), np.float32)

    def put(name, a):
        lo, hi = WEIGHT_COLS[name]
        a = np.asarray(a).reshape(len(a), -1)
        w[:, lo:hi] = np.tile(a, (P // len(a), 1))

    put("dw", np.asarray(L0_conv_w_dw).reshape(GC, KS * KS))
    put("ln_w", np.asarray(L0_conv_ln_w).reshape(GC, 1))
    put("w_off", np.asarray(L0_conv_w_off).T)
    put("wq", np.asarray(L0_conv_wq).reshape(C, G, GC).transpose(2, 1, 0))
    wkvo = np.stack([np.asarray(a) for a in (L0_conv_wk, L0_conv_wv, L0_conv_wo)])
    put("wkvo", wkvo.reshape(3, C, G, GC).transpose(3, 0, 2, 1))
    table = np.zeros((RPAD, G * HG, RPAD), np.float32)
    table[:RPE, :, :RPE] = np.asarray(L0_conv_rpe).transpose(1, 0, 2)
    put("rpe", table)
    put("gate_w", np.asarray(L1_ffn_gate_w).T)
    put("gate_b", np.asarray(L1_ffn_gate_b).reshape(NE, 1))
    put("bias1", np.asarray(L1_ffn_weight1)[:, C, :].T)
    put("bias2", np.asarray(L1_ffn_weight2)[:, HID, :])
    arrays = {
        "x_rows": x_rows,
        "shape_consts": shape_constants(),
        "weights": w,
        "weight1": np.ascontiguousarray(
            np.asarray(L1_ffn_weight1)[:, :C, :].reshape(EQ, E4, C, HID).transpose(1, 2, 0, 3).reshape(P, EQ, HID)),
        "weight2": np.ascontiguousarray(L1_ffn_weight2),
    }
    nc = bacc.Bacc("TRN2", target_bir_lowering=False, num_devices=1)
    args = [nc.dram_tensor(name, a.shape, mybir.dt.from_np(a.dtype), kind="ExternalInput").ap()
            for name, a in arrays.items()]
    y = nc.dram_tensor("y", (NT, P, M), F32, kind="ExternalOutput").ap()
    build(nc, *args, y)
    r = run_bass_kernel_spmd(nc, [arrays], core_ids=[0])
    return np.asarray(r.results[0]["y"]).reshape(B, C, IMG, IMG)
```

```python
from contextlib import ExitStack

import numpy as np

import concourse.bass as bass
from concourse import mybir

F32 = mybir.dt.float32
BF16 = mybir.dt.bfloat16
U32 = mybir.dt.uint32
ALU = mybir.AluOpType
ACT = mybir.ActivationFunctionType
AX = mybir.AxisListType

P = 128
B, C = 8, 32
IMG = 16
M = IMG * IMG
NHALF = M // P
G = 2
GC = C // G
HG = 2
DH = C // (G * HG)
KS, STRIDE, PAD = 5, 4, 2
PADIMG = IMG + 2 * PAD
NK = IMG // STRIDE
N = NK * NK
RPE = 2 * IMG - 1
RPAD = RPE + 1
MAXSHIFT = 4
WIN = IMG + 1 + MAXSHIFT
NE, HID = 16, 128
E4 = P // C
EQ = NE // E4
TOPK = 8
NT = 2
B4 = B // NT
EPS = 1e-5
BUSY = {
    "xn_ready": 45, "off_ready": 28, "off_blk_ready": 34, "hat_rel_ready": 8, "w_smp_ready": 12, "xs_ready": 20,
    "d_prob_ready": 32, "prob_copied": 3, "t1_ready": 46, "t1_copied": 7, "row_tiles": 12, "t2_ready": 90,
    "picked_ready": 35, "picked_copied": 10, "pooled_ready": 9,
}
QK_SCALE = float(DH) ** -0.5
OFFSET = 1.0 / NK * 0.5 * (IMG - 1)
SCORE_BOUND = float(C)


def columns(*widths):
    places, at = {}, 0
    for name, width in widths:
        places[name] = (at, at + width)
        at += width
    return places, at


CONST_COLS, NCONST = columns(
    ("same_b", B), ("eps", 1), ("bound", 1), ("head", HG), ("ref_x", 1), ("at_row", 4), ("at_pixel", 3),
    ("points", 2 * N),
    ("ident", P), ("center", P), ("avg", P),
    ("same_b4", NT * B), ("minus_b4", B4), ("fold", C), ("frac_x", IMG), ("steps", MAXSHIFT),
    ("signs", 4 * MAXSHIFT))
CONST_CUTS = (0, CONST_COLS["ident"][0], CONST_COLS["same_b4"][0], NCONST)

WEIGHT_COLS, NWEIGHT = columns(
    ("wq", G * C), ("dw", KS * KS), ("ln_w", 1), ("w_off", 3), ("wkvo", 3 * G * C), ("rpe", G * HG * RPAD),
    ("gate_w", NE), ("gate_b", 1), ("bias1", NE), ("bias2", C))
WEIGHT_CUT = WEIGHT_COLS["wkvo"][0]


def table_columns():
    half = 0.5 * (IMG - 1)
    at = half * ((0.5 / IMG * 2 - 1) - ((np.arange(NK) + 0.5) / NK * 2 - 1)) + IMG - 1
    least = np.floor(at - OFFSET).astype(int)
    assert (np.floor(at + OFFSET) - least).max() <= MAXSHIFT
    return least.tolist(), at - least


def shape_constants():
    c = np.zeros((P, NCONST), np.float32)

    def put(name, a):
        lo, hi = CONST_COLS[name]
        c[:, lo:hi] = np.broadcast_to(np.asarray(a, np.float64).reshape(len(a), -1), (P, hi - lo))

    p = np.arange(P)
    avg = (p[:, None] // GC == p[None, :] // GC) / GC
    put("avg", avg)
    put("center", np.eye(P) - avg)
    put("ident", np.eye(P))
    put("same_b", p[:, None] // GC == np.arange(B)[None, :])
    put("head", (p[:, None] % GC) // DH == np.arange(HG)[None, :])
    put("eps", np.full((P, 1), EPS))
    put("bound", np.full((P, 1), -SCORE_BOUND))
    ref = (np.arange(NK) + 0.5) / NK * 2 - 1
    ref_y, ref_x = np.repeat(ref, NK), np.tile(ref, NK)
    half = 0.5 * (IMG - 1)
    query = (np.arange(IMG) + 0.5) / IMG * 2 - 1
    put("ref_x", table_columns()[1][p // (P // NK)][:, None])
    put("frac_x", (np.arange(IMG) / IMG)[None, :] * np.ones((P, 1)))
    k = np.arange(1, MAXSHIFT + 1)
    put("steps", k[None, :] * np.ones((P, 1)))
    signs = [np.where(k % bit, 0, np.where(k // bit % 2, 1, -1)) for bit in (4, 2, 1)] + [np.ones(MAXSHIFT)]
    put("signs", np.concatenate(signs)[None, :] * np.ones((P, 1)))
    put("points", half * np.stack([ref_y, ref_x])[None] * np.ones((P, 1, 1)))
    put("at_row", np.stack([half * query[4 * k + p // 32] + IMG - 1 - p % 32 for k in range(4)], 1))
    put("at_pixel", np.stack([p // IMG - half, p // IMG + P // IMG - half, p % IMG - half], 1))
    put("same_b4", (p[:, None] // C + B4 * (np.arange(NT * B) // B)[None, :]) == (np.arange(NT * B) % B)[None, :])
    put("fold", p[:, None] % C == np.arange(C)[None, :])
    put("minus_b4", -1.0 * (p[:, None] // C == np.arange(B4)[None, :]))
    return c


def build(nc, x_in, consts_in, weights_in, w1_in, w2_in, out):
    with ExitStack() as ctx:
        def sb(name, shape, dt=F32):
            return ctx.enter_context(nc.sbuf_tensor(name, shape, dt))

        def sem(name):
            return ctx.enter_context(nc.semaphore(name))

        ps = ctx.enter_context(nc.psum_tensor("ps", [P, 8 * 512], F32))

        def bank(n, cols=512):
            return ps[:, 512 * n:512 * n + cols]

        x_sb = sb("x_sb", [P, G, M])
        cst = sb("cst", [P, NCONST])
        wts = sb("wts", [P, NWEIGHT])
        w1_sb = sb("w1_sb", [P, EQ, HID])
        w2_sb = sb("w2_sb", [HID, NE, C])

        def const(name):
            lo, hi = CONST_COLS[name]
            return cst[:, lo:hi]

        def weight(name):
            lo, hi = WEIGHT_COLS[name]
            return wts[:, lo:hi]

        ident, same_b = const("ident"), const("same_b")
        wq = weight("wq").rearrange("p (g o) -> p g o", g=G)
        wkvo = weight("wkvo").rearrange("p (w g o) -> p w g o", w=3, g=G)

        stats = sb("stats", [P, G, 6])
        meanvar = sb("meanvar", [P, G, 2])
        gn_std = sb("gn_std", [P, G])
        gn_rstd = sb("gn_rstd", [P, G])
        xn = sb("xn", [P, G, M])
        xn_tok = sb("xn_tok", [P, NHALF, G, P])
        wk_s = sb("wk_s", [P, G, C])
        wblk = sb("wblk", [P, 3, G, G, B, GC])
        woblk = sb("woblk", [P, G, B, C])
        gate_blk = sb("gate_blk", [P, NT, B, NE])
        rpe_blk = sb("rpe_blk", [P, G, 4, HG * RPAD])
        q_sb = sb("q_sb", [P, G, M])
        qpad = sb("qpad", [P, G, PADIMG, PADIMG])
        taps = sb("taps", [P, G, NK, NK, KS * KS])
        off = sb("off", [P, G * N])
        off_sq = sb("off_sq", [P, G * N])
        off_std = sb("off_std", [P, G * N])
        off_rstd = sb("off_rstd", [P, G * N])
        off_w = sb("off_w", [P, G * N])
        off_n = sb("off_n", [P, G * N])
        off_act = sb("off_act", [P, G * N])
        off_blk = sb("off_blk", [P, G, B, N])
        warm = sb("warm", [P, 8])
        zeros = sb("zeros", [P, P], BF16)
        th = sb("th", [P, 2, G * B * N])
        half_tanh = sb("half_tanh", [P, G * B * N])
        gate = sb("gate", [P, G * B * N])
        gate_m = sb("gate_m", [P, G, B, N])
        points = sb("points", [P, 2, G * B * N])
        a_rel = sb("a_rel", [P, 4, G * B * N])
        minus_hat_rel = sb("minus_hat_rel", [P, 4, G * B * N])
        a_smp = sb("a_smp", [P, 3, G * B * N])
        minus_hat_smp = sb("minus_hat_smp", [P, 3, G * B * N])
        w_smp = sb("w_smp", [P, NHALF, G * B * N])
        xs = sb("xs", [P, G, B * N])
        kv = sb("kv", [P, 2, G, NT, HG, B4 * N])
        vo = sb("vo", [P, G, NT, B4 * C])
        back_to_n = sb("back_to_n", [P, P])
        txh = sb("txh", [P, G])
        tx = sb("tx", [P, G])
        over = sb("over", [P, G, MAXSHIFT])
        signed = sb("signed", [P, G, 4, MAXSHIFT])
        bits = sb("bits", [P, G, 4])
        masks = sb("masks", [P, G, 4], U32)
        frac = sb("frac", [P, G])
        dist = sb("dist", [P, G, IMG])
        tap_next = sb("tap_next", [P, G, IMG])
        tap_prev = sb("tap_prev", [P, G, IMG])
        tap_both = sb("tap_both", [P, G, IMG])
        tap_here = sb("tap_here", [P, G, IMG])
        win = sb("win", [P, G, IMG * HG, WIN])
        here = sb("here", [P, G, HG, IMG, IMG])
        left = sb("left", [P, G, HG, IMG, IMG])
        right = sb("right", [P, G, HG, IMG, IMG])
        d_max = sb("d_max", [P, NHALF, 32])
        d_sub = sb("d_sub", [P, NHALF, 32, N])
        d_exp = sb("d_exp", [P, NHALF, 32, N])
        d_sum = sb("d_sum", [P, NHALF, 32])
        d_rec = sb("d_rec", [P, NHALF, 32])
        d_prob = sb("d_prob", [P, NHALF, 32, N])
        prob_t = sb("prob_t", [P, NHALF, G, NT, P])
        x1 = sb("x1", [P, NHALF, B, C])
        x2 = sb("x2", [P, NHALF, B, C])
        ln_sum = sb("ln_sum", [P, 2, NHALF, B])
        ln_c = sb("ln_c", [P, 2, NHALF, B, C])
        ln_sq = sb("ln_sq", [P, 2, NHALF, B, C])
        ln_ss = sb("ln_ss", [P, 2, NHALF, B])
        ln_std = sb("ln_std", [P, 2, NHALF, B])
        ln_rstd = sb("ln_rstd", [P, 2, NHALF, B])
        t1 = sb("t1", [P, NHALF, B, C])
        t1_t = sb("t1_t", [P, NT, M])
        e_tok = sb("e_tok", [P, B, NHALF, M])
        e_sum = sb("e_sum", [P, B, NHALF])
        e_rec = sb("e_rec", [P, B, NHALF])
        ot = sb("ot", [P, NT, M])
        o_n = sb("o_n", [P, NHALF, B, C])
        t2 = sb("t2", [P, NHALF, B, C])
        t2_t = sb("t2_t", [P, NT, M])
        g_max = sb("g_max", [P, 1])
        g_exp = sb("g_exp", [P, M])
        g_sum = sb("g_sum", [P, 1])
        g_rec = sb("g_rec", [P, 1])
        g_prob = sb("g_prob", [P, M])
        top = sb("top", [P, TOPK])
        rest = sb("rest", [P, M])
        picked = sb("picked", [P, M])
        picked_t = sb("picked_t", [P, NHALF, P])
        pooled = sb("pooled", [P, EQ, E4, B])
        hidden = sb("hidden", [P, NE, B])
        out2_t = sb("out2_t", [P, B, EQ, E4])
        out2_blk = sb("out2_blk", [P, B, C])
        y_sb = sb("y_sb", [P, NT, M])

        xnt_ps = bank(0).rearrange("p (h g c) -> p h g c", h=NHALF, g=G)
        off_ps = [bank(n, G * B * N) for n in (0, 1, 4)]
        row_ps = [ps[:, 1024 * g:1024 * g + 1024].rearrange("p (r c) -> p r c", c=RPAD) for g in range(G)]
        pt_ps = ps[:, 0:1024].rearrange("p (h g t m) -> p h g t m", h=NHALF, g=G, t=NT)
        t1t_ps = [bank(t, M) for t in range(NT)]
        ot_ps = [bank(t, M) for t in range(NT)]
        y_ps = [bank(t, M) for t in range(NT)]
        q_ps = [bank(2 + g, M) for g in range(G)]
        att_ps = [bank(2 + h, B * C) for h in range(NHALF)]
        t2t_ps = [bank(n, M) for n in (2, 7)]
        g_ps = bank(3, M)
        xs_ps = bank(4, G * P).rearrange("p (g n) -> p g n", g=G)
        kv_ps = [bank(n, G * P).rearrange("p (g n) -> p g n", g=G) for n in (5, 4)]
        vo_ps = bank(5).rearrange("p (g t j) -> p g t j", g=G, t=NT)
        masks_ps = bank(0, G * 4).bitcast(U32).rearrange("p (g k) -> p g k", g=G)
        o_ps = [bank(4 + h, B * C).rearrange("p (b c) -> p b c", b=B) for h in range(NHALF)]
        pickt_ps = bank(4, 256).rearrange("p (h k) -> p h k", h=NHALF)
        out2_ps = bank(4, C)
        pool_ps = bank(5, P)[0:C]
        cen_ps = bank(6, G * N)
        var_ps = bank(7, G * N)
        tx_ps = ps[:, 7 * 512 + 64:7 * 512 + 64 + G]
        lg_ps = ps[:, 3072:4096].rearrange("p (h g t k j) -> p h g t k j", h=NHALF, g=G, t=NT, k=HG)
        hid_ps = bank(6, P).rearrange("p (q e b) -> p q e b", q=EQ, e=E4)
        out2t_ps = bank(7, P).rearrange("p (q e b) -> p q e b", q=EQ, e=E4)
        s_ps = [ps[:, 512 * n:512 * n + 1024] for n in (2, 4, 6, 2)]

        x_loaded = [sem(f"x_loaded{g}") for g in range(G)]
        const_loaded = [sem(f"const_loaded{n}") for n in range(3)]
        weights_loaded = [sem(f"weights_loaded{n}") for n in range(2)]
        w1_loaded, w2_loaded = sem("w1_loaded"), sem("w2_loaded")
        stored = sem("stored")
        dve_step, pool_step, act_step = sem("dve_step"), sem("pool_step"), sem("act_step")
        gn_var_ready, gn_std_ready, xn_ready = sem("gn_var_ready"), sem("gn_std_ready"), sem("xn_ready")
        wq_ready, wkvo_ready, gate_blk_ready = sem("wq_ready"), sem("wkvo_ready"), sem("gate_blk_ready")
        back_to_n_ready = sem("back_to_n_ready")
        rpe_blk_ready, qpad_zeroed = sem("rpe_blk_ready"), sem("qpad_zeroed")
        pooled_zeroed, zeros_set = sem("pooled_zeroed"), sem("zeros_set")
        q_done, qpad_copied, q_copied = sem("q_done"), sem("qpad_copied"), sem("q_copied")
        xn_turned, xn_tok_copied, x1_copied = sem("xn_turned"), sem("xn_tok_copied"), sem("x1_copied")
        off_ready = sem("off_ready")
        centered, squared, var_done = sem("centered"), sem("squared"), sem("var_done")
        off_std_ready, off_n_ready, off_act_ready = sem("off_std_ready"), sem("off_n_ready"), sem("off_act_ready")
        off_blk_ready, off_done = sem("off_blk_ready"), sem("off_done")
        tanh_ready, txh_ready, half_tanh_ready = sem("tanh_ready"), sem("txh_ready"), sem("half_tanh_ready")
        points_ready, a_rel_ready = sem("points_ready"), sem("a_rel_ready")
        a_smp_ready = sem("a_smp_ready")
        w_smp_ready, gate_m_ready = sem("w_smp_ready"), sem("gate_m_ready")
        hat_rel_ready, masks_ready, taps_ready = sem("hat_rel_ready"), sem("masks_ready"), sem("taps_ready")
        sampled, xs_ready = sem("sampled"), sem("xs_ready")
        k_done, v_done, k_ready, v_ready = sem("k_done"), sem("v_done"), sem("k_ready"), sem("v_ready")
        vo_done, vo_copied = sem("vo_done"), sem("vo_copied")
        rows_done, win_copied, rows_used = sem("rows_done"), sem("win_copied"), sem("rows_used")
        shifts_done, left_edge_zeroed = sem("shifts_done"), sem("left_edge_zeroed")
        sides_ready = sem("sides_ready")
        here_ready = [sem(f"here_ready{g}") for g in range(G)]
        logits_done, d_sub_ready = sem("logits_done"), sem("d_sub_ready")
        d_exp_ready, d_rec_ready = sem("d_exp_ready"), sem("d_rec_ready")
        d_prob_ready = [sem(f"d_prob_ready{h}") for h in range(NHALF)]
        prob_turned, prob_copied, att_done = sem("prob_turned"), sem("prob_copied"), sem("att_done")
        ln_c_ready, ln_sq_ready, ln_ss_ready, ln_std_ready = (
            sem("ln_c_ready"), sem("ln_sq_ready"), sem("ln_ss_ready"), sem("ln_std_ready"))
        t1_ready, t1_turned = sem("t1_ready"), sem("t1_turned")
        t1_copied = [sem(f"t1_copied{t}") for t in range(NT)]
        scores_done, exp_ready = sem("scores_done"), sem("exp_ready")
        ot_done, ot_copied, o_turned, x2_ready = sem("ot_done"), sem("ot_copied"), sem("o_turned"), sem("x2_ready")
        t2_ready, t2_turned, g_done = sem("t2_ready"), sem("t2_turned"), sem("g_done")
        t2_copied = [sem(f"t2_copied{t}") for t in range(NT)]
        g_max_ready, g_exp_ready = sem("g_max_ready"), sem("g_exp_ready")
        picked_ready, picked_turned, picked_copied = sem("picked_ready"), sem("picked_turned"), sem("picked_copied")
        pooled_done, pooled_ready, hidden_done = sem("pooled_done"), sem("pooled_ready"), sem("hidden_done")
        hidden_ready = sem("hidden_ready")
        out2t_done, out2t_copied, out2_done, out2_ready = (
            sem("out2t_done"), sem("out2t_copied"), sem("out2_done"), sem("out2_ready"))
        y_done, y_ready = sem("y_done"), sem("y_ready")

        def conv_view(g, i):
            rows = qpad[:, g, STRIDE * i:STRIDE * i + KS, :]
            return bass.AP(tensor=rows.tensor, offset=rows.offset,
                           ap=[list(rows.ap[0]), [STRIDE, NK], [PADIMG, KS], [1, KS]])

        block = ctx.enter_context(nc.Block())

        def tap(engine, product, g, shift, weights, x0=0):
            return engine.tensor_tensor(
                product[:, g, :, :, x0:], win[:, g, :, x0 + shift:IMG + shift].rearrange("p (y h) x -> p h y x", h=HG),
                weights[:, g, x0:].unsqueeze(1).unsqueeze(1).to_broadcast([P, HG, IMG, IMG - x0]), ALU.mult)

        def by_denominator(engine, h):
            return engine.tensor_tensor(d_prob[:, h], d_exp[:, h], d_rec[:, h].unsqueeze(2).to_broadcast([P, 32, N]),
                                        ALU.mult)

        @block.sync
        def _(sp):
            def load_const(n):
                cols = slice(CONST_CUTS[n], CONST_CUTS[n + 1])
                sp.dma_start(cst[:, cols], consts_in[:, cols]).then_inc(const_loaded[n], 16)

            sp.dma_start(x_sb[:, 0, :], x_in[0]).then_inc(x_loaded[0], 16)
            load_const(0)
            load_const(1)
            sp.dma_start(wts[:, WEIGHT_CUT:], weights_in[:, WEIGHT_CUT:]).then_inc(weights_loaded[1], 16)
            load_const(2)
            sp.dma_start(w1_sb[:, :, :], w1_in).then_inc(w1_loaded, 16)
            sp.wait_ge(y_ready, 1)
            sp.dma_start(out[0], y_sb[:, 0, :]).then_inc(stored, 16)
            sp.wait_ge(stored, 32)

        @block.gpsimd
        def _(pool):
            steps = [0]

            def link(ins):
                steps[0] += 1
                ins.then_inc(pool_step, 1)
                pool.wait_ge(pool_step, steps[0])

            nc.gpsimd.memset(qpad[:, :, :, :], 0.0).then_inc(qpad_zeroed, 1)
            nc.gpsimd.memset(left[:, :, :, :, 0:1], 0.0).then_inc(left_edge_zeroed, 1)
            nc.gpsimd.memset(pooled[:, :, :, :], 0.0).then_inc(pooled_zeroed, 1)

            def blocks(dst, src, n_groups, width):
                return nc.gpsimd.tensor_tensor(
                    dst, src.unsqueeze(2).to_broadcast([P, n_groups, B, width]),
                    same_b.unsqueeze(1).unsqueeze(3).to_broadcast([P, n_groups, B, width]), ALU.mult)

            pool.wait_ge(weights_loaded[0], 16)
            pool.wait_ge(const_loaded[0], 16)
            blocks(wblk[:, 0, 1], wq[:, 1].rearrange("p (g o) -> p g o", g=G), G, GC).then_inc(wq_ready, 1)
            pool.wait_ge(weights_loaded[1], 16)
            pool.wait_ge(const_loaded[2], 16)
            same_b4 = const("same_b4").rearrange("p (t b) -> p t b", t=NT)
            rpe = weight("rpe").rearrange("p (g k) -> p g k", g=G)
            nc.gpsimd.tensor_tensor(
                rpe_blk[:, :, :, :], rpe.unsqueeze(2).to_broadcast([P, G, 4, HG * RPAD]),
                const("minus_b4").unsqueeze(1).unsqueeze(3).to_broadcast([P, G, 4, HG * RPAD]),
                ALU.mult).then_inc(rpe_blk_ready, 1)
            link(nc.gpsimd.tensor_scalar(wk_s[:, :, :], wkvo[:, 0], QK_SCALE, None, ALU.mult))
            for g in range(G):
                blocks(wblk[:, 1, g], wk_s[:, g].rearrange("p (g o) -> p g o", g=G), G, GC).then_inc(wkvo_ready, 1)
                blocks(wblk[:, 2, g], wkvo[:, 1, g].rearrange("p (g o) -> p g o", g=G), G, GC).then_inc(wkvo_ready, 1)
            pool.wait_ge(const_loaded[1], 16)
            nc.gpsimd.tensor_copy(back_to_n[:, :].rearrange("p (r x) -> p x r", x=NK),
                                  ident.rearrange("p (x r) -> p x r", x=NK)).then_inc(back_to_n_ready, 1)
            pool.wait_ge(masks_ready, 1)
            link(nc.gpsimd.tensor_tensor(frac[:, :], tx[:, :], bits[:, :, 3], ALU.subtract))
            link(nc.gpsimd.tensor_tensor(dist[:, :, :], frac[:, :].unsqueeze(2).to_broadcast([P, G, IMG]),
                                         const("frac_x").unsqueeze(1).to_broadcast([P, G, IMG]), ALU.subtract))
            nc.gpsimd.tensor_scalar(tap_next[:, :, :], dist[:, :, :], 0.0, None, ALU.max)
            link(nc.gpsimd.tensor_scalar(tap_prev[:, :, :], dist[:, :, :], -1.0, 0.0, ALU.mult, ALU.max))
            link(nc.gpsimd.tensor_tensor(tap_both[:, :, :], tap_next[:, :, :], tap_prev[:, :, :], ALU.add))
            nc.gpsimd.tensor_scalar(tap_here[:, :, :], tap_both[:, :, :], -1.0, 1.0, ALU.mult,
                                    ALU.add).then_inc(taps_ready, 1)
            pool.wait_ge(half_tanh_ready, 1)
            link(nc.gpsimd.tensor_scalar(gate[:, :], half_tanh[:, :], 0.5, 0.5, ALU.mult, ALU.add))
            for g in range(G):
                nc.gpsimd.tensor_tensor(
                    gate_m[:, g], gate[:, :].rearrange("p (g b n) -> p g b n", g=G, b=B)[:, g],
                    same_b.unsqueeze(2).to_broadcast([P, B, N]), ALU.mult).then_inc(gate_m_ready, 1)
            for g in range(G):
                blocks(woblk[:, g].unsqueeze(1), wkvo[:, 2, g].unsqueeze(1), 1, C).then_inc(wkvo_ready, 1)
            pool.wait_ge(shifts_done, 1)
            pool.wait_ge(taps_ready, 1)
            tap(nc.gpsimd, left, 0, -1, tap_prev, 1)
            link(tap(nc.gpsimd, right, 0, 1, tap_next))
            nc.gpsimd.tensor_tensor(left[:, 0], left[:, 0], right[:, 0], ALU.add).then_inc(sides_ready, 1)
            tap(nc.gpsimd, here, 0, 0, tap_here).then_inc(here_ready[0], 1)
            pool.wait_ge(d_rec_ready, 1)
            by_denominator(nc.gpsimd, 0).then_inc(d_prob_ready[0], 1)
            nc.gpsimd.tensor_tensor(
                gate_blk[:, :, :, :], weight("gate_w").unsqueeze(1).unsqueeze(1).to_broadcast([P, NT, B, NE]),
                same_b4.unsqueeze(3).to_broadcast([P, NT, B, NE]), ALU.mult).then_inc(gate_blk_ready, 1)

        @block.scalar
        def _(act):
            act.dma_start(x_sb[:, 1, :], x_in[1]).then_inc(x_loaded[1], 16)
            act.dma_start(wts[:, 0:WEIGHT_CUT], weights_in[:, 0:WEIGHT_CUT]).then_inc(weights_loaded[0], 16)
            warmed = [0]

            def load_table(func):
                n = warmed[0]
                warmed[0] += 1
                nc.scalar.activation(warm[:, n:n + 1], zeros[:, 0:1], func)

            act.wait_ge(zeros_set, 1)
            load_table(ACT.Sqrt)
            act.dma_start(w2_sb[:, :, :], w2_in[:, 0:HID, :].rearrange("e h o -> h e o")).then_inc(w2_loaded, 16)
            act.wait_ge(const_loaded[0], 16)
            act.wait_ge(gn_var_ready, 1)
            nc.scalar.activation(gn_std[:, :], meanvar[:, :, 1], ACT.Sqrt, bias=const("eps")).then_inc(gn_std_ready, 1)
            act.wait_ge(qpad_zeroed, 1)
            for g in range(G):
                act.wait_ge(q_done, g + 1)
                nc.scalar.activation(qpad[:, g, PAD:PAD + IMG, PAD:PAD + IMG],
                                     q_ps[g].rearrange("p (y x) -> p y x", y=IMG), ACT.Copy).then_inc(qpad_copied, 1)
            for g in range(G):
                nc.scalar.activation(q_sb[:, g], q_ps[g], ACT.Copy).then_inc(q_copied, 1)
            act.wait_ge(xn_turned, 1)
            nc.scalar.activation(xn_tok[:, :, :, :], xnt_ps, ACT.Copy).then_inc(xn_tok_copied, 1)
            act.wait_ge(centered, 1)
            nc.scalar.activation(off_sq[:, :], cen_ps, ACT.Square).then_inc(squared, 1)
            act.wait_ge(var_done, 1)
            nc.scalar.activation(off_std[:, :], var_ps, ACT.Sqrt, bias=const("eps")).then_inc(off_std_ready, 1)
            load_table(ACT.Gelu)
            act.wait_ge(off_n_ready, 1)
            nc.scalar.activation(off_act[:, :], off_n[:, :], ACT.Gelu).then_inc(off_act_ready, 1)
            for j in range(2):
                act.wait_ge(off_done, j + 1)
                nc.scalar.activation(th[:, j], off_ps[j], ACT.Tanh).then_inc(tanh_ready, 1)
            act.wait_ge(off_done, 3)
            nc.scalar.activation(txh[:, :], tx_ps, ACT.Tanh).then_inc(txh_ready, 1)

            def distance(a, k, axis, place):
                act.wait_ge(points_ready, axis + 1)
                return nc.scalar.activation(a[:, k], points[:, axis], ACT.Abs, bias=const(place)[:, k:k + 1],
                                            scale=-1.0)

            for k in range(4):
                distance(a_rel, k, 0, "at_row").then_inc(a_rel_ready, 1)
            for k in range(3):
                distance(a_smp, k, 0 if k < NHALF else 1, "at_pixel").then_inc(a_smp_ready, 1)
            act.wait_ge(off_done, 4)
            nc.scalar.activation(half_tanh[:, :], off_ps[2], ACT.Tanh, scale=0.5).then_inc(half_tanh_ready, 1)
            for g in range(G):
                act.wait_ge(rows_done, g + 1)
                nc.scalar.activation(win[:, g], row_ps[g][:, :, 0:WIN], ACT.Copy).then_inc(win_copied, 1)
            load_table(ACT.Exp)
            for w, done, ready in ((0, k_done, k_ready), (1, v_done, v_ready)):
                act.wait_ge(done, 1)
                for hh in range(HG):
                    nc.scalar.activation(kv[:, w, :, :, hh], kv_ps[w].rearrange("p g (t j) -> p g t j", t=NT), ACT.Copy,
                                         scale=const("head")[:, hh:hh + 1]).then_inc(ready, 1)
            act.wait_ge(d_sub_ready, 1)
            nc.scalar.activation(d_exp[:, 0], d_sub[:, 0], ACT.Exp).then_inc(d_exp_ready, 1)
            act.wait_ge(d_sub_ready, 2)
            nc.scalar.activation(d_exp[:, 1], d_sub[:, 1], ACT.Exp).then_inc(d_exp_ready, 1)
            act.wait_ge(vo_done, 1)
            nc.scalar.activation(vo[:, :, :, :], vo_ps, ACT.Copy).then_inc(vo_copied, 1)
            load_table(ACT.Sqrt)
            for h in range(NHALF):
                act.wait_ge(prob_turned, h + 1)
                nc.scalar.activation(prob_t[:, h], pt_ps[:, h], ACT.Copy).then_inc(prob_copied, 1)

            def layernorm(k):
                for h in range(NHALF):
                    act.wait_ge(ln_c_ready, NHALF * k + h + 1)
                    nc.scalar.activation(ln_sq[:, k, h], ln_c[:, k, h], ACT.Square).then_inc(ln_sq_ready, 1)
                    if k == 0:
                        nc.scalar.activation(x1[:, h].rearrange("p b c -> p (b c)"), att_ps[h],
                                             ACT.Copy).then_inc(x1_copied, 1)
                for h in range(NHALF):
                    act.wait_ge(ln_ss_ready, NHALF * k + h + 1)
                    nc.scalar.activation(ln_std[:, k, h], ln_ss[:, k, h], ACT.Sqrt, bias=const("eps"),
                                         scale=1.0 / C).then_inc(ln_std_ready, 1)

            layernorm(0)
            load_table(ACT.Exp)
            act.wait_ge(t1_turned, 1)
            nc.scalar.activation(t1_t[:, 0], t1t_ps[0], ACT.Copy).then_inc(t1_copied[0], 1)
            for n in range(B // 2):
                act.wait_ge(scores_done, n + 1)
                parts = 1 if n < B // 2 - 1 else 2
                for k in range(parts):
                    cols = slice(k * 1024 // parts, (k + 1) * 1024 // parts)
                    pair = e_tok[:, 2 * n:2 * n + 2].rearrange("p b h q -> p (b h q)")
                    nc.scalar.activation(pair[:, cols], s_ps[n][:, cols], ACT.Exp,
                                         bias=const("bound")).then_inc(exp_ready, 1)
                if n == 2:
                    act.wait_ge(ot_done, 1)
                    nc.scalar.activation(ot[:, 0], ot_ps[0], ACT.Copy).then_inc(ot_copied, 1)
            act.wait_ge(ot_done, 2)
            nc.scalar.activation(ot[:, 1], ot_ps[1], ACT.Copy).then_inc(ot_copied, 1)
            load_table(ACT.Sqrt)
            layernorm(1)
            load_table(ACT.Exp)
            act.wait_ge(t2_turned, 1)
            nc.scalar.activation(t2_t[:, 0], t2t_ps[0], ACT.Copy).then_inc(t2_copied[0], 1)
            act.wait_ge(g_max_ready, 1)
            nc.scalar.activation(g_exp[:, :], g_ps, ACT.Exp, bias=g_max[:, 0:1],
                                 accum_out=g_sum[:, 0:1]).then_inc(g_exp_ready, 1)
            load_table(ACT.Gelu)
            act.wait_ge(hidden_done, 1)
            nc.scalar.activation(hidden[:, :, :], hid_ps.rearrange("p q e b -> p (q e) b"),
                                 ACT.Gelu).then_inc(hidden_ready, 1)
            act.wait_ge(y_done, 2)
            nc.scalar.activation(y_sb[:, 1, :], y_ps[1], ACT.Copy).then_inc(act_step, 1)
            act.wait_ge(act_step, 1)
            act.dma_start(out[1], y_sb[:, 1, :]).then_inc(stored, 16)

        @block.tensor
        def _(pe):
            mm = nc.tensor.matmul

            def nx_rows(nx):
                return slice(nx * P // NK, (nx + 1) * P // NK)

            def keep_busy(wait, n_bank):
                for _ in range(BUSY[wait]):
                    mm(bank(n_bank, P), zeros[:, :], zeros[:, :], start=True, stop=True)

            pe.wait_ge(zeros_set, 1)
            keep_busy("xn_ready", 7)
            pe.wait_ge(wq_ready, 2)
            pe.wait_ge(xn_ready, 2)
            for g in range(G):
                for gi in range(G):
                    last = mm(q_ps[g], wblk[:, 0, gi, g].rearrange("p b o -> p (b o)"), xn[:, gi],
                              start=(gi == 0), stop=(gi == G - 1))
                last.then_inc(q_done, 1)
            pe.wait_ge(const_loaded[1], 16)
            for h in range(NHALF):
                for g in range(G):
                    last = nc.tensor.transpose(xnt_ps[:, h, g], xn[:, g, h * P:(h + 1) * P], ident)
            last.then_inc(xn_turned, 1)
            keep_busy("off_ready", 7)
            pe.wait_ge(off_ready, G)
            mm(cen_ps, const("center"), off[:, :], start=True, stop=True).then_inc(centered, 1)
            pe.wait_ge(squared, 1)
            mm(var_ps, const("avg"), off_sq[:, :], start=True, stop=True).then_inc(var_done, 1)
            keep_busy("off_blk_ready", 4)
            pe.wait_ge(off_blk_ready, 1)
            pe.wait_ge(xn_tok_copied, 1)
            cols = off_blk[:, :, :, :].rearrange("p g b n -> p (g b n)")

            def offset(j):
                return mm(off_ps[j], weight("w_off")[:, j:j + 1].to_broadcast([P, P]), cols, start=True, stop=True)

            offset(0).then_inc(off_done, 1)
            offset(1).then_inc(off_done, 1)
            for g in range(G):
                for nx in range(NK):
                    last = mm(tx_ps[nx_rows(nx), g:g + 1], off_blk[:, g].rearrange("p b n -> p (b n)")[:, nx::NK],
                              weight("w_off")[:, 1:2], start=True, stop=True)
            last.then_inc(off_done, 1)
            offset(2).then_inc(off_done, 1)
            keep_busy("hat_rel_ready", 5)
            pe.wait_ge(rpe_blk_ready, 1)
            pe.wait_ge(q_copied, G)
            for g in range(G):
                for yq in range(4):
                    pe.wait_ge(hat_rel_ready, yq + 1)
                    for nx, least in enumerate(table_columns()[0]):
                        last = mm(row_ps[g][nx_rows(nx), 8 * yq:8 * yq + 8, 0:WIN],
                                  minus_hat_rel[:, yq, g * P + nx:(g + 1) * P:NK],
                                  rpe_blk[:, g].rearrange("p k (h c) -> p (k h) c", h=HG)[:, :, least:least + WIN],
                                  start=True, stop=True)
                last.then_inc(rows_done, 1)
            keep_busy("w_smp_ready", 5)
            pe.wait_ge(half_tanh_ready, 1)
            pe.wait_ge(w_smp_ready, 2)
            for g in range(G):
                for h in range(NHALF):
                    last = mm(xs_ps[:, g], xn_tok[:, h, g], w_smp[:, h, g * P:(g + 1) * P],
                              start=(h == 0), stop=(h == NHALF - 1))
            last.then_inc(sampled, 1)
            keep_busy("xs_ready", 6)
            pe.wait_ge(xs_ready, 1)
            pe.wait_ge(wkvo_ready, 4)
            for w, done in ((0, k_done), (1, v_done)):
                for g in range(G):
                    for gi in range(G):
                        last = mm(kv_ps[w][:, g], wblk[:, 1 + w, gi, g].rearrange("p b o -> p (b o)"), xs[:, gi],
                                  start=(gi == 0), stop=(gi == G - 1))
                last.then_inc(done, 1)

            def turn_on(part, g, h):
                for hh in range(HG):
                    last = mm(lg_ps[:, h, g, :, hh], part[:, g, hh, 8 * h:8 * h + 8].rearrange("p y x -> p (y x)"),
                              back_to_n[:, :].rearrange("p (t j) -> p t j", t=NT), start=False, stop=True,
                              skip_group_check=True)
                return last

            pe.wait_ge(k_ready, HG)
            pe.wait_ge(txh_ready, 1)
            for h in range(NHALF):
                for g in range(G):
                    mm(lg_ps[:, h, g].rearrange("p t k j -> p (t k j)"), q_sb[:, g, h * P:(h + 1) * P],
                       kv[:, 0, g].rearrange("p t k j -> p (t k j)"),
                       start=(g == 0), stop=False, skip_group_check=True)
            pe.wait_ge(rows_used, 1)
            pe.wait_ge(back_to_n_ready, 1)
            pe.wait_ge(sides_ready, 1)
            for h in range(NHALF):
                turn_on(left, 0, h)
            for h in range(NHALF):
                for g in range(G):
                    pe.wait_ge(here_ready[g], 1)
                    last = turn_on(here, g, h)
                last.then_inc(logits_done, 1)
            pe.wait_ge(rows_used, G)
            for h in range(NHALF):
                for g in range(G):
                    mm(att_ps[h].rearrange("p (b g c) -> p g b c", b=B, g=G)[:, g], x_sb[:, g, h * P:(h + 1) * P],
                       ident, start=(g == 0), stop=False, skip_group_check=True)
            pe.wait_ge(v_ready, HG)
            pe.wait_ge(wkvo_ready, 6)
            for g in range(G):
                for t in range(NT):
                    last = mm(vo_ps[:, g, t], kv[:, 1, g, t].rearrange("p k j -> p (k j)"),
                              woblk[:, g, B4 * t:B4 * t + B4].rearrange("p b o -> p (b o)"),
                              start=True, stop=True)
            last.then_inc(vo_done, 1)
            keep_busy("d_prob_ready", 0)
            for h in range(NHALF):
                pe.wait_ge(d_prob_ready[h], 1)
                for g in range(G):
                    for t in range(NT):
                        first = 2 * B * g + B * t
                        last = nc.tensor.transpose(
                            pt_ps[:, h, g, t], d_prob[:, h, first:first + B].rearrange("p b n -> p (b n)"), ident)
                last.then_inc(prob_turned, 1)
            keep_busy("prob_copied", 4)
            pe.wait_ge(vo_copied, 1)
            for h in range(NHALF):
                pe.wait_ge(prob_copied, h + 1)
                for t in range(NT):
                    for g in range(G):
                        last = mm(att_ps[h][:, P * t:P * t + P], prob_t[:, h, g, t], vo[:, g, t],
                                  start=False, stop=(g == G - 1), skip_group_check=True)
                last.then_inc(att_done, 1)
            t1_rows = t1[:, :, :, :].rearrange("p h b c -> p h (b c)")
            keep_busy("t1_ready", 6)
            pe.wait_ge(t1_ready, NHALF)
            for t in range(NT):
                for h in range(NHALF):
                    last = nc.tensor.transpose(t1t_ps[t][:, h * P:(h + 1) * P], t1_rows[:, h, P * t:P * t + P], ident)
                last.then_inc(t1_turned, 1)

            def scores(n):
                t = n // 2
                pe.wait_ge(t1_copied[t], 1)
                for h in range(NHALF):
                    for b in (2 * n, 2 * n + 1):
                        rows = slice(C * (b % B4), C * (b % B4) + C)
                        last = mm(s_ps[n][:, 512 * (b % 2) + M * h:512 * (b % 2) + M * h + M],
                                  t1_t[rows, t, h * P:(h + 1) * P], t1_t[rows, t, :], start=(h == 0), stop=True,
                                  skip_group_check=True)
                last.then_inc(scores_done, 1)

            def attend(n):
                for b in (2 * n, 2 * n + 1):
                    pe.wait_ge(exp_ready, n + 1 if n < B // 2 - 1 else b - B // 2 + 2)
                    for h in range(NHALF):
                        rows = slice(C * (b % B4), C * (b % B4) + C)
                        last = mm(ot_ps[b // B4][rows], t1[:, h, b], e_tok[:, b, h],
                                  start=(h == 0), stop=(h == NHALF - 1))
                if n % 2 == 1:
                    last.then_inc(ot_done, 1)

            def turn_back(t):
                pe.wait_ge(ot_copied, t + 1)
                for h in range(NHALF):
                    last = nc.tensor.transpose(bank(4 + h)[:, t * P:(t + 1) * P], ot[:, t, h * P:(h + 1) * P], ident)
                last.then_inc(o_turned, 1)

            keep_busy("t1_copied", 6)
            pe.wait_ge(x1_copied, NHALF)
            scores(0)
            pe.wait_ge(t1_copied[1], 1)
            scores(1)
            keep_busy("row_tiles", 1)
            scores(2)
            attend(0)
            scores(3)
            attend(1)
            attend(2)
            attend(3)
            turn_back(0)
            turn_back(1)
            keep_busy("t2_ready", 6)
            t2_rows = t2[:, :, :, :].rearrange("p h b c -> p h (b c)")
            for h in range(NHALF):
                pe.wait_ge(t2_ready, h + 1)
                for t in range(NT):
                    turned = nc.tensor.transpose(t2t_ps[t][:, h * P:(h + 1) * P], t2_rows[:, h, P * t:P * t + P], ident)
                    if h == NHALF - 1:
                        turned.then_inc(t2_turned, 1)
            mm(g_ps, ident, weight("gate_b").to_broadcast([P, M]), start=True, stop=False)
            pe.wait_ge(gate_blk_ready, 1)
            for t in range(NT):
                pe.wait_ge(t2_copied[t], 1)
                last = mm(g_ps, gate_blk[:, t].rearrange("p b e -> p (b e)"), t2_t[:, t],
                          start=False, stop=(t == NT - 1))
            last.then_inc(g_done, 1)
            x2_rows = x2[:, :, :, :].rearrange("p h b c -> p h (b c)")
            for t in range(NT):
                for h in range(NHALF):
                    mm(y_ps[t][:, h * P:(h + 1) * P], x2_rows[:, h, P * t:P * t + P], ident,
                       start=(h == 0), stop=False, skip_group_check=True)
            keep_busy("picked_ready", 6)
            pe.wait_ge(picked_ready, 1)
            for h in range(NHALF):
                last = nc.tensor.transpose(pickt_ps[:, h], picked[:, h * P:(h + 1) * P], ident)
            last.then_inc(picked_turned, 1)
            keep_busy("picked_copied", 6)
            pe.wait_ge(picked_copied, 1)
            for b in range(B):
                for h in range(NHALF):
                    last = mm(pool_ps[:, NE * b:NE * b + NE], t2[:, h, b, :], picked_t[:, h, NE * b:NE * b + NE],
                              start=(h == 0), stop=(h == NHALF - 1))
            last.then_inc(pooled_done, 1)
            mm(hid_ps.rearrange("p q e b -> p (q e) b"), ident, weight("bias1").unsqueeze(2).to_broadcast([P, NE, B]),
               start=True, stop=False, skip_group_check=True)
            pe.wait_ge(w1_loaded, 16)
            keep_busy("pooled_ready", 7)
            pe.wait_ge(pooled_ready, E4)
            for q in range(EQ):
                last = mm(hid_ps[:, q].rearrange("p e b -> p (e b)"), w1_sb[:, q, :],
                          pooled[:, q].rearrange("p e b -> p (e b)"), start=False, stop=True,
                          skip_group_check=True)
            last.then_inc(hidden_done, 1)
            pe.wait_ge(hidden_ready, 1)
            pe.wait_ge(w2_loaded, 16)
            for q in range(EQ):
                experts = slice(E4 * q, E4 * q + E4)
                last = mm(out2t_ps[:, q].rearrange("p e b -> p (e b)"), w2_sb[:, experts].rearrange("p e o -> p (e o)"),
                          hidden[:, experts].rearrange("p e b -> p (e b)"), start=True, stop=True)
            last.then_inc(out2t_done, 1)
            mm(out2_ps, ident, weight("bias2"), start=True, stop=False)
            pe.wait_ge(out2t_copied, 1)
            mm(out2_ps, out2_t[:, :, :, :].rearrange("p b q e -> p (b q e)"), const("fold"),
               start=False, stop=True).then_inc(out2_done, 1)
            for t in range(NT):
                pe.wait_ge(out2_ready, t + 1)
                mm(y_ps[t], out2_blk[:, B4 * t:B4 * t + B4].rearrange("p b o -> p (b o)"), picked[:, :],
                   start=False, stop=True, skip_group_check=True).then_inc(y_done, 1)

        @block.vector
        def _(dve):
            steps = [0]

            def link(ins):
                steps[0] += 1
                ins.then_inc(dve_step, 1)
                dve.wait_ge(dve_step, steps[0])

            tt = nc.vector.tensor_tensor
            ts = nc.vector.tensor_scalar
            stt = nc.vector.scalar_tensor_tensor
            reduce = nc.vector.tensor_reduce

            nc.vector.memset(zeros[:, :], 0.0).then_inc(zeros_set, 1)
            for g in range(G):
                dve.wait_ge(x_loaded[g], 16)
                link(nc.vector.bn_stats(stats[:, g], x_sb[:, g]))
                last = nc.vector.bn_aggr(meanvar[:, g], stats[:, g])
            last.then_inc(gn_var_ready, 1)
            dve.wait_ge(weights_loaded[0], 16)
            dve.wait_ge(const_loaded[0], 16)
            tt(wblk[:, 0, 0],
               wq[:, 0].rearrange("p (g o) -> p g o", g=G).unsqueeze(2).to_broadcast([P, G, B, GC]),
               same_b.unsqueeze(1).unsqueeze(3).to_broadcast([P, G, B, GC]), ALU.mult).then_inc(wq_ready, 1)
            dve.wait_ge(gn_std_ready, 1)
            link(nc.vector.reciprocal(gn_rstd[:, :], gn_std[:, :]))
            for g in range(G):
                ts(xn[:, g], x_sb[:, g], meanvar[:, g, 0:1], gn_rstd[:, g:g + 1], ALU.subtract,
                   ALU.mult).then_inc(xn_ready, 1)
            dw = weight("dw").rearrange("p (a b) -> p a b", a=KS).unsqueeze(1).to_broadcast([P, NK, KS, KS])
            for g in range(G):
                dve.wait_ge(qpad_copied, g + 1)
                for i in range(NK):
                    last = tt(taps[:, g, i].rearrange("p j (a b) -> p j a b", a=KS), conv_view(g, i), dw, ALU.mult)
                link(last)
                reduce(off[:, g * N:(g + 1) * N], taps[:, g].rearrange("p i j k -> p (i j) k"), AX.X,
                       ALU.add).then_inc(off_ready, 1)
            dve.wait_ge(off_ready, G)
            ts(off_w[:, :], off[:, :], weight("ln_w"), None, ALU.mult)
            dve.wait_ge(off_std_ready, 1)
            link(nc.vector.reciprocal(off_rstd[:, :], off_std[:, :]))
            tt(off_n[:, :], off_w[:, :], off_rstd[:, :], ALU.mult).then_inc(off_n_ready, 1)
            dve.wait_ge(off_act_ready, 1)
            tt(off_blk[:, :, :, :],
               off_act[:, :].rearrange("p (g n) -> p g n", g=G).unsqueeze(2).to_broadcast([P, G, B, N]),
               same_b.unsqueeze(1).unsqueeze(3).to_broadcast([P, G, B, N]), ALU.mult).then_inc(off_blk_ready, 1)

            for axis in range(2):
                dve.wait_ge(tanh_ready, axis + 1)
                stt(out=points[:, axis].rearrange("p (q n) -> p q n", n=N),
                    in0=th[:, axis].rearrange("p (q n) -> p q n", n=N), scalar=OFFSET,
                    in1=const("points")[:, axis * N:(axis + 1) * N].unsqueeze(1).to_broadcast([P, G * B, N]),
                    op0=ALU.mult, op1=ALU.add).then_inc(points_ready, 1)
            for k in range(4):
                dve.wait_ge(a_rel_ready, k + 1)
                ts(minus_hat_rel[:, k], a_rel[:, k], -1.0, 0.0, ALU.add, ALU.min).then_inc(hat_rel_ready, 1)
            dve.wait_ge(const_loaded[2], 16)
            dve.wait_ge(txh_ready, 1)
            link(ts(tx[:, :], txh[:, :], -OFFSET, const("ref_x"), ALU.mult, ALU.add))
            link(tt(over[:, :, :], tx[:, :].unsqueeze(2).to_broadcast([P, G, MAXSHIFT]),
                    const("steps").unsqueeze(1).to_broadcast([P, G, MAXSHIFT]), ALU.is_ge))
            link(tt(signed[:, :, :, :], over[:, :, :].unsqueeze(2).to_broadcast([P, G, 4, MAXSHIFT]),
                    const("signs").rearrange("p (k j) -> p k j", k=4).unsqueeze(1).to_broadcast([P, G, 4, MAXSHIFT]),
                    ALU.mult))
            link(reduce(bits[:, :, :], signed[:, :, :, :], AX.X, ALU.add))
            nc.vector.tensor_copy(masks[:, :, :], bits[:, :, :]).then_inc(masks_ready, 1)
            dve.wait_ge(masks_ready, 1)
            dve.wait_ge(a_smp_ready, 3)
            link(ts(minus_hat_smp[:, :, :], a_smp[:, :, :], -1.0, 0.0, ALU.add, ALU.min))
            for h in range(NHALF):
                tt(w_smp[:, h], minus_hat_smp[:, h], minus_hat_smp[:, 2], ALU.mult).then_inc(w_smp_ready, 1)

            def shifts(g):
                dve.wait_ge(win_copied, g + 1)

                def shifted(width, bit, source, mask):
                    return nc.vector.copy_predicated(
                        win[:, g, :, 0:width], mask[:, g, bit:bit + 1].unsqueeze(2).to_broadcast(
                            [P, IMG * HG, width]), source)

                shifted(IMG + 1, 0, row_ps[g][:, :, 4:WIN], masks).then_inc(rows_used, 1)
                dve.wait_ge(rows_used, g + 1)
                if g == 0:
                    link(nc.vector.tensor_copy(masks_ps, masks[:, :, :]))
                link(shifted(IMG + 2, 1, win[:, g, :, 2:IMG + 4], masks_ps))
                shifted(IMG + 1, 2, win[:, g, :, 1:IMG + 2], masks_ps).then_inc(shifts_done, 1)
                dve.wait_ge(shifts_done, g + 1)

            shifts(0)
            dve.wait_ge(sampled, 1)
            dve.wait_ge(gate_m_ready, G)
            tt(xs[:, :, :], xs_ps, gate_m[:, :, :, :].rearrange("p g b n -> p g (b n)"), ALU.mult).then_inc(xs_ready, 1)
            shifts(1)
            dve.wait_ge(taps_ready, 1)
            dve.wait_ge(left_edge_zeroed, 1)
            tap(nc.vector, left, 1, -1, tap_prev, 1)
            tap(nc.vector, right, 1, 1, tap_next)
            link(tap(nc.vector, here, 1, 0, tap_here))
            link(tt(left[:, 1], left[:, 1], right[:, 1], ALU.add))
            tt(here[:, 1], here[:, 1], left[:, 1], ALU.add).then_inc(here_ready[1], 1)
            lg_rows = [lg_ps[:, h].rearrange("p g t k (b n) -> p (g t k b) n", n=N) for h in range(NHALF)]
            for h in range(NHALF):
                dve.wait_ge(logits_done, h + 1)
                link(reduce(d_max[:, h], lg_rows[h], AX.X, ALU.max))
                tt(d_sub[:, h], lg_rows[h], d_max[:, h].unsqueeze(2).to_broadcast([P, 32, N]),
                   ALU.subtract).then_inc(d_sub_ready, 1)
            for h in range(NHALF):
                dve.wait_ge(d_exp_ready, h + 1)
                link(reduce(d_sum[:, h], d_exp[:, h], AX.X, ALU.add))
                if h == 0:
                    nc.vector.reciprocal(d_rec[:, h], d_sum[:, h]).then_inc(d_rec_ready, 1)
                else:
                    link(nc.vector.reciprocal(d_rec[:, h], d_sum[:, h]))
                    by_denominator(nc.vector, h).then_inc(d_prob_ready[h], 1)

            def by_token(a):
                return a.unsqueeze(2).to_broadcast([P, B, C])

            def center(k, h, src):
                stt(out=ln_c[:, k, h], in0=by_token(ln_sum[:, k, h]), scalar=-1.0 / C, in1=src, op0=ALU.mult,
                    op1=ALU.add).then_inc(ln_c_ready, 1)

            def normalize(k, dst, ready):
                for h in range(NHALF):
                    dve.wait_ge(ln_sq_ready, NHALF * k + h + 1)
                    reduce(ln_ss[:, k, h], ln_sq[:, k, h], AX.X, ALU.add).then_inc(ln_ss_ready, 1)
                for h in range(NHALF):
                    dve.wait_ge(ln_std_ready, NHALF * k + h + 1)
                    dve.wait_ge(ln_c_ready, NHALF * k + h + 1)
                    link(nc.vector.reciprocal(ln_rstd[:, k, h], ln_std[:, k, h]))
                    tt(dst[:, h], ln_c[:, k, h], by_token(ln_rstd[:, k, h]), ALU.mult).then_inc(ready, 1)

            for h in range(NHALF):
                dve.wait_ge(att_done, h + 1)
                result = att_ps[h].rearrange("p (b c) -> p b c", b=B)
                link(reduce(ln_sum[:, 0, h], result, AX.X, ALU.add))
                center(0, h, result)
            normalize(0, t1, t1_ready)
            dve.wait_ge(t1_turned, 2)
            nc.vector.tensor_copy(t1_t[:, 1], t1t_ps[1]).then_inc(t1_copied[1], 1)
            for n in range(B // 2 - 1):
                dve.wait_ge(exp_ready, n + 1)
                reduce(e_sum[:, 2 * n:2 * n + 2], e_tok[:, 2 * n:2 * n + 2], AX.X, ALU.add)
            for b in (B - 2, B - 1):
                dve.wait_ge(exp_ready, b - B // 2 + 2)
                last = reduce(e_sum[:, b], e_tok[:, b], AX.X, ALU.add)
            link(last)
            link(nc.vector.reciprocal(e_rec[:, :, :], e_sum[:, :, :]))
            dve.wait_ge(o_turned, NT)
            dve.wait_ge(x1_copied, NHALF)
            for h in range(NHALF):
                last = tt(o_n[:, h], o_ps[h], by_token(e_rec[:, :, h]), ALU.mult)
            link(last)
            for h in range(NHALF):
                tt(x2[:, h], x1[:, h], o_n[:, h], ALU.add).then_inc(x2_ready, 1)
            for h in range(NHALF):
                dve.wait_ge(x2_ready, h + 1)
                last = reduce(ln_sum[:, 1, h], x2[:, h], AX.X, ALU.add)
            link(last)
            for h in range(NHALF):
                center(1, h, x2[:, h])
            normalize(1, t2, t2_ready)
            dve.wait_ge(t2_turned, NT)
            nc.vector.tensor_copy(t2_t[:, 1], t2t_ps[1]).then_inc(t2_copied[1], 1)
            dve.wait_ge(g_done, 1)
            reduce(g_max[:, :], g_ps, AX.X, ALU.max, negate=True).then_inc(g_max_ready, 1)
            dve.wait_ge(g_exp_ready, 1)
            link(nc.vector.reciprocal(g_rec[:, :], g_sum[:, :]))
            link(ts(g_prob[:, :], g_exp[:, :], g_rec[:, 0:1], None, ALU.mult))
            link(nc.vector.max(top[:, :], g_prob[:, :]))
            link(nc.vector.match_replace(rest[:, :], top[:, :], g_prob[:, :], 0.0))
            tt(picked[:, :], g_prob[:, :], rest[:, :], ALU.subtract).then_inc(picked_ready, 1)
            dve.wait_ge(picked_turned, 1)
            nc.vector.tensor_copy(picked_t[:, :, :], pickt_ps).then_inc(picked_copied, 1)
            dve.wait_ge(pooled_zeroed, 1)
            dve.wait_ge(pooled_done, 1)
            for e in range(E4):
                nc.vector.tensor_copy(
                    pooled[C * e:C * e + C, :, e, :],
                    pool_ps.rearrange("p (b q e) -> p e q b", q=EQ, e=E4)[:, e]).then_inc(pooled_ready, 1)
            dve.wait_ge(out2t_done, 1)
            tt(out2_t[:, :, :, :].rearrange("p b q e -> p q e b"), out2t_ps,
               const("same_b4")[:, 0:E4].unsqueeze(1).unsqueeze(3).to_broadcast([P, EQ, E4, B]),
               ALU.mult).then_inc(out2t_copied, 1)
            dve.wait_ge(out2_done, 1)
            for t in range(NT):
                batches = slice(B4 * t, B4 * t + B4)
                tt(out2_blk[:, batches], out2_ps.unsqueeze(1).to_broadcast([P, B4, C]),
                   same_b[:, batches].unsqueeze(2).to_broadcast([P, B4, C]), ALU.mult).then_inc(out2_ready, 1)
            dve.wait_ge(y_done, 1)
            nc.vector.tensor_copy(y_sb[:, 0, :], y_ps[0]).then_inc(y_ready, 1)


def kernel(x, L0_conv_w_dw, L0_conv_ln_w, L0_conv_w_off, L0_conv_wq, L0_conv_wk, L0_conv_wv, L0_conv_wo, L0_conv_rpe,
           L1_ffn_gate_w, L1_ffn_gate_b, L1_ffn_weight1, L1_ffn_weight2):
    import concourse.bacc as bacc
    from concourse.bass_utils import run_bass_kernel_spmd

    x_rows = np.ascontiguousarray(np.asarray(x).reshape(B, G, GC, M).transpose(1, 0, 2, 3).reshape(G, P, M))
    w = np.zeros((P, NWEIGHT), np.float32)

    def put(name, a):
        lo, hi = WEIGHT_COLS[name]
        a = np.asarray(a).reshape(len(a), -1)
        w[:, lo:hi] = np.tile(a, (P // len(a), 1))

    put("dw", np.asarray(L0_conv_w_dw).reshape(GC, KS * KS))
    put("ln_w", np.asarray(L0_conv_ln_w).reshape(GC, 1))
    put("w_off", np.asarray(L0_conv_w_off).T)
    put("wq", np.asarray(L0_conv_wq).reshape(C, G, GC).transpose(2, 1, 0))
    wkvo = np.stack([np.asarray(a) for a in (L0_conv_wk, L0_conv_wv, L0_conv_wo)])
    put("wkvo", wkvo.reshape(3, C, G, GC).transpose(3, 0, 2, 1))
    table = np.zeros((RPAD, G * HG, RPAD), np.float32)
    table[:RPE, :, :RPE] = np.asarray(L0_conv_rpe).transpose(1, 0, 2)
    put("rpe", table)
    put("gate_w", np.asarray(L1_ffn_gate_w).T)
    put("gate_b", np.asarray(L1_ffn_gate_b).reshape(NE, 1))
    put("bias1", np.asarray(L1_ffn_weight1)[:, C, :].T)
    put("bias2", np.asarray(L1_ffn_weight2)[:, HID, :])
    arrays = {
        "x_rows": x_rows,
        "shape_consts": shape_constants(),
        "weights": w,
        "weight1": np.ascontiguousarray(
            np.asarray(L1_ffn_weight1)[:, :C, :].reshape(EQ, E4, C, HID).transpose(1, 2, 0, 3).reshape(P, EQ, HID)),
        "weight2": np.ascontiguousarray(L1_ffn_weight2),
    }
    nc = bacc.Bacc("TRN2", target_bir_lowering=False, num_devices=1)
    args = [nc.dram_tensor(name, a.shape, mybir.dt.from_np(a.dtype), kind="ExternalInput").ap()
            for name, a in arrays.items()]
    y = nc.dram_tensor("y", (NT, P, M), F32, kind="ExternalOutput").ap()
    build(nc, *args, y)
    r = run_bass_kernel_spmd(nc, [arrays], core_ids=[0])
    return np.asarray(r.results[0]["y"]).reshape(B, C, IMG, IMG)
```
